# Optimizing a Trainium2 kernel written in Bass

```python
import numpy as np
import jax
import jax.numpy as jnp

def _softmax(x, axis=-1):
    return jax.nn.softmax(x, axis=axis)

def _gelu(x):
    return jax.nn.gelu(x, approximate=True)

def _silu(x):
    return jax.nn.silu(x)

def _sigmoid(x):
    return jax.nn.sigmoid(x)

def _layernorm(x, axis=-1, eps=1e-05):
    m = jnp.mean(x, axis=axis, keepdims=True)
    v = jnp.var(x, axis=axis, keepdims=True)
    return (x - m) / jnp.sqrt(v + eps)

def _scatter_add(tgt, idx, src, axis=0):
    return tgt.at[idx].add(src)

def _segment_sum(src, seg, n):
    return jax.ops.segment_sum(src, seg, n)
kernel_name = 'mk_perceiver_d1_seqx_r4_5a2f39'

def setup_inputs(seed: int=0):
    np.random.seed(seed)
    _w = jnp.asarray

    def _rec_inputs():
        import jax
        import jax.numpy as jnp
        _rk = jax.random.key(seed)
        x = -0.0003929 + 0.9999 * jax.random.normal(jax.random.fold_in(_rk, 1), (2, 256, 512), jnp.float32)
        _lenS = 256 - jax.random.randint(jax.random.fold_in(_rk, 7), (2,), 0, max(1, 256 // 4) + 1, jnp.int32)
        _lenS2 = 4096 - jax.random.randint(jax.random.fold_in(_rk, 8), (2,), 0, max(1, 4096 // 4) + 1, jnp.int32)
        _ctx_2048P = jax.random.normal(jax.random.fold_in(_rk, 11), (2, 16, 512), jnp.float32)
        _ctx_2048c = jax.random.dirichlet(jax.random.fold_in(_rk, 511), 0.3 * jnp.ones((16,), jnp.float32), (2, 4096))
        _ctx_2048t = jnp.einsum('bsk,bkd->bsd', _ctx_2048c, _ctx_2048P)
        _ctx_2048t = _ctx_2048t * jax.lax.rsqrt(jnp.mean(jnp.square(_ctx_2048t)) + 1e-12) * 0.953939
        ctx_2048 = -1.39393e-06 + 0.999914 * (_ctx_2048t + 0.3 * jax.random.normal(jax.random.fold_in(_rk, 611), (2, 4096, 512), jnp.float32))
        itok_BxS_0_1023 = jax.random.randint(jax.random.fold_in(_rk, 12), (2, 256), 0, 256, jnp.int32)
        return (x, ctx_2048, itok_BxS_0_1023)
    x, ctx_2048, itok_BxS_0_1023 = _rec_inputs()

    def _L0_xattn_setup():
        import jax, jax.numpy as jnp
        import numpy as np
        B, Lq, Lk = (2, 1024, 256)
        Q_DIM, KV_DIM = (512, 512)
        H, HD = (16, 128)
        KVC, QC, R = (128, 192, 64)
        LOOKBACK = 8
        NEG = -1e+30

        def _rope(x, L):
            half = x.shape[-1] // 2
            inv_freq = 1.0 / 10000.0 ** (jnp.arange(half, dtype=jnp.float32) / half)
            ang = jnp.arange(L, dtype=jnp.float32)[:, None] * inv_freq
            cos, sin = (jnp.cos(ang), jnp.sin(ang))
            x1, x2 = (x[..., :half], x[..., half:])
            return jnp.concatenate([x1 * cos - x2 * sin, x1 * sin + x2 * cos], axis=-1)
        key = jax.random.key(seed)
        ks = jax.random.split(key, 11)

        def w(k, shape, fan_in):
            return jax.random.normal(k, shape, jnp.float32) / np.sqrt(fan_in).astype(np.float32)
        return {'q': jax.random.normal(ks[0], (B, Lq, Q_DIM), jnp.float32), 'kv': jax.random.normal(ks[1], (B, Lk, KV_DIM), jnp.float32), 'seg_id': jnp.sort(jax.random.randint(ks[2], (B, Lq), 0, Lk), axis=-1), 'W_kvc': w(ks[3], (KV_DIM, KVC), KV_DIM), 'W_dq': w(ks[4], (Q_DIM, QC), Q_DIM), 'W_uq': w(ks[5], (QC, H * HD), QC), 'W_qr': w(ks[6], (QC, H * R), QC), 'W_uk': w(ks[7], (KVC, H * HD), KVC), 'W_kr': w(ks[8], (KVC, R), KVC), 'W_uv': w(ks[9], (KVC, H * HD), KVC), 'W_o': w(ks[10], (H * HD, Q_DIM), H * HD)}
    _L0_xattn_all = _L0_xattn_setup()
    _L0_xattn_in = {k: v for k, v in _L0_xattn_all.items() if k in ('W_kvc', 'W_dq', 'W_uq', 'W_qr', 'W_uk', 'W_kr', 'W_uv', 'W_o')}
    del _L0_xattn_all

    def _L0_attn_setup():
        import jax, jax.numpy as jnp
        import numpy as np
        B, T, C = (2, 512, 512)
        NH, NKV, HD = (16, 8, 64)
        SOFTCAP = 50.0
        ROPE_BASE = 10000.0

        def _rotate_half(x):
            x1, x2 = (x[..., :x.shape[-1] // 2], x[..., x.shape[-1] // 2:])
            return jnp.concatenate((-x2, x1), axis=-1)

        def _rope_cos_sin(t, head_dim, dtype):
            inv_freq = 1.0 / ROPE_BASE ** (jnp.arange(0, head_dim, 2, dtype=jnp.int32).astype(jnp.float32) / head_dim)
            pos = jnp.arange(t, dtype=jnp.float32)
            freqs = pos[:, None] * inv_freq[None, :]
            emb = jnp.concatenate((freqs, freqs), axis=-1)
            return (jnp.cos(emb).astype(dtype)[None, None], jnp.sin(emb).astype(dtype)[None, None])
        key = jax.random.key(seed)
        ks = jax.random.split(key, 5)
        s = 0.02
        return {'X': jax.random.normal(ks[0], (B, T, C), dtype=jnp.float32), 'Wq': jax.random.normal(ks[1], (C, NH * HD), dtype=jnp.float32) * s, 'Wk': jax.random.normal(ks[2], (C, NKV * HD), dtype=jnp.float32) * s, 'Wv': jax.random.normal(ks[3], (C, NKV * HD), dtype=jnp.float32) * s, 'Wo': jax.random.normal(ks[4], (NH * HD, C), dtype=jnp.float32) * s}
    _L0_attn_all = _L0_attn_setup()
    _L0_attn_in = {k: v for k, v in _L0_attn_all.items() if k in ('Wq', 'Wk', 'Wv', 'Wo')}
    del _L0_attn_all

    def _L0_ffn_setup():
        import jax, jax.numpy as jnp
        import numpy as np
        FP8_MAX = 448.0
        GLOBAL_DIV = 448.0 * 6.0

        def _fp8(x):
            return x.astype(jnp.float8_e4m3fn).astype(jnp.float32)

        def _reorder_quantize_x(x, idx):
            scale = jnp.max(jnp.abs(x)) / GLOBAL_DIV
            xr = (x / scale)[:, idx]
            scale_x = jnp.max(jnp.abs(xr), axis=1, keepdims=True) / FP8_MAX
            qx = _fp8(xr / scale_x)
            return (qx, scale_x, scale)

        def _qlinear(qx, scale_x, scale, W, idx, out_idx=None):
            Wr = W[:, idx]
            w_scale = jnp.max(jnp.abs(Wr), axis=1, keepdims=True) / FP8_MAX
            qw = _fp8(Wr / w_scale)
            y = qx * scale_x @ (qw * w_scale).T * scale
            if out_idx is not None:
                y = y[:, out_idx]
            return y
        key = jax.random.key(seed)
        ks = jax.random.split(key, 6)
        B, S, H, I = (2, 256, 512, 1408)
        return {'x': jax.random.normal(ks[0], (B, S, H), jnp.float32), 'w_gate': jax.random.normal(ks[1], (I, H), jnp.float32) * 0.02, 'w_up': jax.random.normal(ks[2], (I, H), jnp.float32) * 0.02, 'w_down': jax.random.normal(ks[3], (H, I), jnp.float32) * 0.02, 'up_reorder_index': jax.random.permutation(ks[4], jnp.arange(H, dtype=jnp.int64)), 'down_reorder_index': jax.random.permutation(ks[5], jnp.arange(I, dtype=jnp.int64))}
    _L0_ffn_all = _L0_ffn_setup()
    _L0_ffn_in = {k: v for k, v in _L0_ffn_all.items() if k in ('w_gate', 'w_up', 'w_down', 'up_reorder_index', 'down_reorder_index')}
    del _L0_ffn_all
    return {'x': x, 'ctx_2048': ctx_2048, 'itok_BxS_0_1023': itok_BxS_0_1023, 'L0_xattn_W_kvc': _L0_xattn_in['W_kvc'], 'L0_xattn_W_dq': _L0_xattn_in['W_dq'], 'L0_xattn_W_uq': _L0_xattn_in['W_uq'], 'L0_xattn_W_qr': _L0_xattn_in['W_qr'], 'L0_xattn_W_uk': _L0_xattn_in['W_uk'], 'L0_xattn_W_kr': _L0_xattn_in['W_kr'], 'L0_xattn_W_uv': _L0_xattn_in['W_uv'], 'L0_xattn_W_o': _L0_xattn_in['W_o'], 'L0_attn_Wq': _L0_attn_in['Wq'], 'L0_attn_Wk': _L0_attn_in['Wk'], 'L0_attn_Wv': _L0_attn_in['Wv'], 'L0_attn_Wo': _L0_attn_in['Wo'], 'L0_ffn_w_gate': _L0_ffn_in['w_gate'], 'L0_ffn_w_up': _L0_ffn_in['w_up'], 'L0_ffn_w_down': _L0_ffn_in['w_down'], 'L0_ffn_up_reorder_index': _L0_ffn_in['up_reorder_index'], 'L0_ffn_down_reorder_index': _L0_ffn_in['down_reorder_index']}

def reference(x, ctx_2048, itok_BxS_0_1023, L0_xattn_W_kvc, L0_xattn_W_dq, L0_xattn_W_uq, L0_xattn_W_qr, L0_xattn_W_uk, L0_xattn_W_kr, L0_xattn_W_uv, L0_xattn_W_o, L0_attn_Wq, L0_attn_Wk, L0_attn_Wv, L0_attn_Wo, L0_ffn_w_gate, L0_ffn_w_up, L0_ffn_w_down, L0_ffn_up_reorder_index, L0_ffn_down_reorder_index):
    import jax
    import jax.numpy as jnp

    def _L0_xattn_ref(q, kv, seg_id, W_kvc, W_dq, W_uq, W_qr, W_uk, W_kr, W_uv, W_o):
        import jax, jax.numpy as jnp
        import numpy as np
        B, Lq, Lk = (2, 1024, 256)
        Q_DIM, KV_DIM = (512, 512)
        H, HD = (16, 128)
        KVC, QC, R = (128, 192, 64)
        LOOKBACK = 8
        NEG = -1e+30

        def _rope(x, L):
            half = x.shape[-1] // 2
            inv_freq = 1.0 / 10000.0 ** (jnp.arange(half, dtype=jnp.float32) / half)
            ang = jnp.arange(L, dtype=jnp.float32)[:, None] * inv_freq
            cos, sin = (jnp.cos(ang), jnp.sin(ang))
            x1, x2 = (x[..., :half], x[..., half:])
            return jnp.concatenate([x1 * cos - x2 * sin, x1 * sin + x2 * cos], axis=-1)
        b, lq, _ = q.shape
        lk = kv.shape[1]
        kv_c = kv @ W_kvc
        q_c = q @ W_dq
        q_nope = (q_c @ W_uq).reshape(b, lq, H, HD).transpose(0, 2, 1, 3)
        q_rope = (q_c @ W_qr).reshape(b, lq, H, R).transpose(0, 2, 1, 3)
        k_nope = (kv_c @ W_uk).reshape(b, lk, H, HD)
        v = (kv_c @ W_uv).reshape(b, lk, H, HD)
        k_rope = kv_c @ W_kr
        q_rope = _rope(q_rope, lq)
        k_rope = _rope(k_rope, lk)
        scale = 1.0 / np.sqrt(HD + R).astype(np.float32)
        scores = (jnp.einsum('bhqd,bkhd->bhqk', q_nope, k_nope) + jnp.einsum('bhqr,bkr->bhqk', q_rope, k_rope)) * scale
        k_ids = jnp.arange(lk)[None, None, :]
        qs = seg_id[:, :, None]
        good = (k_ids <= qs) & (k_ids >= qs - LOOKBACK)
        scores = jnp.where(good[:, None, :, :], scores, NEG)
        attn = jax.nn.softmax(scores, axis=-1)
        out = jnp.einsum('bhqk,bkhd->bqhd', attn, v).reshape(b, lq, H * HD)
        return out @ W_o

    def _L0_attn_ref(X, Wq, Wk, Wv, Wo):
        import jax, jax.numpy as jnp
        import numpy as np
        B, T, C = (2, 512, 512)
        NH, NKV, HD = (16, 8, 64)
        SOFTCAP = 50.0
        ROPE_BASE = 10000.0

        def _rotate_half(x):
            x1, x2 = (x[..., :x.shape[-1] // 2], x[..., x.shape[-1] // 2:])
            return jnp.concatenate((-x2, x1), axis=-1)

        def _rope_cos_sin(t, head_dim, dtype):
            inv_freq = 1.0 / ROPE_BASE ** (jnp.arange(0, head_dim, 2, dtype=jnp.int32).astype(jnp.float32) / head_dim)
            pos = jnp.arange(t, dtype=jnp.float32)
            freqs = pos[:, None] * inv_freq[None, :]
            emb = jnp.concatenate((freqs, freqs), axis=-1)
            return (jnp.cos(emb).astype(dtype)[None, None], jnp.sin(emb).astype(dtype)[None, None])
        b, t, c = X.shape
        n_rep = NH // NKV
        q = (X @ Wq).reshape(b, t, NH, HD).transpose(0, 2, 1, 3)
        k = (X @ Wk).reshape(b, t, NKV, HD).transpose(0, 2, 1, 3)
        v = (X @ Wv).reshape(b, t, NKV, HD).transpose(0, 2, 1, 3)
        cos, sin = _rope_cos_sin(t, HD, X.dtype)
        q = q * cos + _rotate_half(q) * sin
        k = k * cos + _rotate_half(k) * sin
        k = jnp.repeat(k, n_rep, axis=1)
        v = jnp.repeat(v, n_rep, axis=1)
        scale = 256.0 ** (-0.5)
        att = jnp.einsum('bhqd,bhkd->bhqk', q, k) * scale
        att = SOFTCAP * jnp.tanh(att / SOFTCAP)
        causal = jnp.tril(jnp.ones((t, t), dtype=bool))
        att = jnp.where(causal[None, None], att, -jnp.inf)
        att = jax.nn.softmax(att, axis=-1)
        y = jnp.einsum('bhqk,bhkd->bhqd', att, v)
        y = y.transpose(0, 2, 1, 3).reshape(b, t, NH * HD)
        return y @ Wo

    def _L0_ffn_ref(x, w_gate, w_up, w_down, up_reorder_index, down_reorder_index):
        import jax, jax.numpy as jnp
        import numpy as np
        FP8_MAX = 448.0
        GLOBAL_DIV = 448.0 * 6.0

        def _fp8(x):
            return x.astype(jnp.float8_e4m3fn).astype(jnp.float32)

        def _reorder_quantize_x(x, idx):
            scale = jnp.max(jnp.abs(x)) / GLOBAL_DIV
            xr = (x / scale)[:, idx]
            scale_x = jnp.max(jnp.abs(xr), axis=1, keepdims=True) / FP8_MAX
            qx = _fp8(xr / scale_x)
            return (qx, scale_x, scale)

        def _qlinear(qx, scale_x, scale, W, idx, out_idx=None):
            Wr = W[:, idx]
            w_scale = jnp.max(jnp.abs(Wr), axis=1, keepdims=True) / FP8_MAX
            qw = _fp8(Wr / w_scale)
            y = qx * scale_x @ (qw * w_scale).T * scale
            if out_idx is not None:
                y = y[:, out_idx]
            return y
        B, S, H = x.shape
        xf = x.reshape(B * S, H)
        qx, sx, sc = _reorder_quantize_x(xf, up_reorder_index)
        g = _qlinear(qx, sx, sc, w_gate, up_reorder_index, out_idx=down_reorder_index)
        u = _qlinear(qx, sx, sc, w_up, up_reorder_index, out_idx=down_reorder_index)
        t = jax.nn.silu(g) * u
        qt, st, sct = _reorder_quantize_x(t, down_reorder_index)
        y = _qlinear(qt, st, sct, w_down, down_reorder_index)
        return y.reshape(B, S, H)
    x = x + _L0_xattn_ref(_layernorm(x, axis=-1), ctx_2048, itok_BxS_0_1023, L0_xattn_W_kvc, L0_xattn_W_dq, L0_xattn_W_uq, L0_xattn_W_qr, L0_xattn_W_uk, L0_xattn_W_kr, L0_xattn_W_uv, L0_xattn_W_o)
    x = x + _L0_attn_ref(_layernorm(x, axis=-1), L0_attn_Wq, L0_attn_Wk, L0_attn_Wv, L0_attn_Wo)
    x = x + _L0_ffn_ref(_layernorm(x, axis=-1), L0_ffn_w_gate, L0_ffn_w_up, L0_ffn_w_down, L0_ffn_up_reorder_index, L0_ffn_down_reorder_index)
    return x

_drawn_inputs = setup_inputs


def setup_inputs(seed=0):
    import zlib

    import numpy as np

    out = dict(_drawn_inputs(seed))
    spreads = {}
    factors = {'L0_attn_Wq': 8.0, 'L0_attn_Wk': 8.0}
    for name, (base, spread) in spreads.items():
        noise = np.random.default_rng([zlib.crc32(name.encode()), seed]).standard_normal(out[name].shape)
        drawn = base * np.exp(spread * noise) if base else spread * noise
        out[name] = jnp.asarray(drawn.astype(out[name].dtype))
    for name, factor in factors.items():
        out[name] = (out[name] * factor).astype(out[name].dtype)
    return out
```

```python
from contextlib import ExitStack, contextmanager

import numpy as np
import concourse.bass as bass
from concourse import mybir

F32 = mybir.dt.float32
BF16 = mybir.dt.bfloat16
I32 = mybir.dt.int32
U32 = mybir.dt.uint32
ALU = mybir.AluOpType
ACT = mybir.ActivationFunctionType
AX = mybir.AxisListType

P = 128
B, S, D = 2, 256, 512
LK = 4096
NT = B * S // P
TPB = S // P
DC = D // P
H, HD, KVC, QC, R = 16, 128, 128, 192, 64
QLO, QHI = P, QC - P
LOOKBACK = 8
WIN = LOOKBACK + 1
GQ = P // H
NG = P // GQ
GK = WIN * GQ
GN = 96
XSCALE = 1.0 / float(np.sqrt(np.float32(HD + R)))
NEG = -1e30
NH, NKV, AD = 16, 8, 64
REP = NH // NKV
SOFTCAP = 50.0
ASCALE = 256.0 ** -0.5
VW = 96
FI = 1408
FT = FI // NT
FCH = [(0, 128), (128, 128), (256, 96)]
NFC = NT * len(FCH)
FP8_MAX = 448.0
FCOLS = [(0, 512), (512, 512), (1024, 384)]
EPS = 1e-5


class Line:

    def __init__(self, name, sem, step):
        self.name, self.sem, self.step, self.n, self.base = name, sem, step, 0, 0


class Mark:

    def __init__(self, line, n, path):
        self.line, self.n, self.path = line, n, path


class Counter:
    def __init__(self, nc, es, plan):
        self.nc, self.es, self.plan = nc, es, plan
        self.new = {"K": {}, "opened": {}}
        self.lines, self.gates, self.stack, self.iters = {}, [], [], {}
        self.seen = {}
        self.eng = {"PE": nc.tensor, "ACT": nc.scalar, "DVE": nc.vector, "POOL": nc.gpsimd, "SP": nc.sync}
        self.spare = es.enter_context(nc.semaphore("s_spare"))
        for e in ("PE", "ACT", "DVE", "POOL"):
            self.line(e, 1)

    def line(self, name, step, software=False):
        assert not self.stack, "a line has to be made outside of the loops"
        ln = Line(name, self.es.enter_context(self.nc.semaphore("s_" + name)), step)
        self.lines[name] = ln
        off = 0 if software else max([k.get(name, 0) for k in self.plan["K"].values()] + [0])
        if off:
            self.nc.sync.sem_inc(ln.sem, off)
        ln.base = off
        return ln

    @property
    def path(self):
        return tuple(x[0] for x in self.stack)

    def done(self, line, ins, *gates):
        ln = self.lines[line]
        ins.then_inc(ln.sem, ln.step)
        ln.n += ln.step
        m = Mark(ln, ln.n, self.path)
        for g in gates:
            g.opened[-1][line] = m
        return m

    def wait(self, engs, *gates):
        for e in engs.split():
            for g in gates:
                for d in range(len(g.opened) - 1, -1, -1):
                    for m in g.opened[d].values():
                        self.wait_mark(e, m)
                    if g.opened[d]:
                        break
                    if d > 0:
                        for m in self.plan["opened"].get(self.stack[d - 1][0], {}).get(g.name, {}).values():
                            self.wait_mark(e, m, prev=True)

    def wait_mark(self, eng, mark, prev=False):
        key = (eng, mark.line.name, mark.path, prev)
        if self.seen.get(key, -1) >= mark.n:
            return
        self.seen[key] = mark.n
        ln = self.lines[mark.line.name]
        v = mark.n + ln.base
        active = {x[0]: x[1] for x in self.stack}
        expr = None
        for lp in mark.path:
            k = self.plan["K"].get(lp, {}).get(mark.line.name, 0)
            if lp in active:
                if k:
                    expr = active[lp] * k if expr is None else expr + active[lp] * k
            else:
                v += (self.iters[lp] - 1) * k
        if prev:
            v -= self.plan["K"].get(mark.path[-1], {}).get(mark.line.name, 0)
        self.eng[eng].wait_ge(ln.sem, v if expr is None else expr + v)

    def hold(self, *engs):
        for e in engs:
            self.eng[e].sem_inc(self.spare, 1)

    @contextmanager
    def loop(self, name, n):
        if self.stack:
            self.hold(*self.eng)
        start = {k: ln.n for k, ln in self.lines.items()}
        with self.nc.Fori(0, n) as i:
            self.iters[name] = n
            self.stack.append((name, i))
            self.seen = {}
            for g in self.gates:
                g.opened.append({})
            yield i
            self.new["opened"][name] = {}
            for g in self.gates:
                inner = g.opened.pop()
                if inner:
                    self.new["opened"][name][g.name] = inner
                    g.opened[-1].update(inner)
            self.stack.pop()
            self.seen = {}
        ks = {}
        for k, ln in self.lines.items():
            d = ln.n - start.get(k, ln.n)
            ks[k] = d
            ln.n += d * (n - 1)
        self.new["K"][name] = ks


class Gate:

    def __init__(self, c, name):
        self.name = name
        self.opened = [{} for _ in range(len(c.stack) + 1)]
        c.gates.append(self)


class Buf:

    def __init__(self, c, name, t):
        self.c, self.name, self.t = c, name, t
        self.full, self.free = Gate(c, name + " full"), Gate(c, name + " free")

    def __getitem__(self, k):
        return self.t[k]


class Ring:

    def __init__(self, bufs):
        self.bufs, self.i, self.depth = bufs, 0, None

    def take(self):
        c = self.bufs[0].c
        if self.depth != c.path:
            self.depth, self.i = c.path, 0
        b = self.bufs[self.i % len(self.bufs)]
        self.i += 1
        return b


def build(nc, a, out, plan):
    with ExitStack() as es:
        c = Counter(nc, es, plan)
        T, A, V, G, SP = nc.tensor, nc.scalar, nc.vector, nc.gpsimd, nc.sync

        def sb(name, shape, dt=F32, scope=None):
            return Buf(c, name, (scope or es).enter_context(nc.sbuf_tensor(name, shape, dt)))

        banks = Ring([Buf(c, f"ps{i}", es.enter_context(nc.psum_tensor(f"ps{i}", [P, 512], F32))) for i in range(7)])
        psO = Buf(c, "psO", es.enter_context(nc.psum_tensor("psO", [P, 512], F32)))

        def dma_line(buf, software=False):
            ln = "d_" + buf.name
            if ln not in c.lines:
                c.line(ln, 16, software)
            return ln

        def load(buf, dst, src, eng="SP"):
            ln = dma_line(buf)
            h = c.eng[eng]
            with nc.allow_non_contiguous_dma(reason="strided weight or index layouts"):
                return c.done(ln, h.dma_start(dst, src), buf.full)

        wait, done = c.wait, c.done

        turn = [0]

        def evac(dst, dst_ap, bank, bank_ap, eng=None):
            if eng is None:
                eng = ("ACT", "DVE")[turn[0] % 2]
                turn[0] += 1
            wait(eng, bank.full)
            if eng == "ACT":
                ins = A.activation(dst_ap, bank_ap, ACT.Copy)
            else:
                ins = V.tensor_copy(dst_ap, bank_ap)
            return done(eng, ins, dst.full, bank.free)

        ident = sb("ident", [P, P])
        x1 = sb("x1", [P, NT * D])
        tab = sb("tab", [P, NT * P])
        half = sb("half", [P, 1])
        hN = sb("hN", [P, D])
        hT = sb("hT", [P, D])
        st = sb("st", [P, 12])
        wq = sb("wq", [P, DC * NH * AD])

        load(ident, ident[:], a["eye"])
        load(x1, x1[:].rearrange("p (t d) -> p t d", t=NT), a["x"].rearrange("b (t p) d -> p (b t) d", p=P))
        done("POOL", G.memset(half[:], -0.5), half.full)

        def layer_norm(xin):
            wait("DVE", x1.full)
            wait("POOL", half.full)
            wait("DVE", st.free)
            done("DVE", V.bn_stats(st[:, 0:6], xin), st.full)
            wait("DVE", st.full)
            c.hold("DVE")
            done("DVE", V.bn_aggr(st[:, 6:8], st[:, 0:6]), st.full)
            wait("DVE", st.full)
            done("DVE", V.tensor_scalar(st[:, 8:9], st[:, 7:8], EPS, None, ALU.add), st.full)
            wait("POOL", st.full)
            done("POOL", G.tensor_tensor(st[:, 9:10], st[:, 8:9], half[:], ALU.pow), st.full)
            wait("DVE", hN.free)
            wait("DVE", st.full)
            m = done("DVE", V.tensor_scalar(hN[:], xin, st[:, 6:7], st[:, 9:10], ALU.subtract, ALU.mult), hN.full, st.free, x1.free)

        def transpose_h():
            ps = banks.take()
            wait("PE", ps.free)
            wait("PE", hN.full)
            wait("PE", ident.full)
            for k in range(DC):
                ins = T.transpose(ps[:, k * P:(k + 1) * P], hN[:, k * P:(k + 1) * P], ident[:])
            done("PE", ins, ps.full, hN.free)
            wait("ACT", hT.free)
            evac(hT, hT[:], ps, ps[:], "ACT")

        def matmuls(parts, *gates):
            for o, terms in parts:
                for n, (l, rh) in enumerate(terms):
                    ins = T.matmul(o, l, rh, start=n == 0, stop=n == len(terms) - 1)
            return done("PE", ins, *gates)

        def rope(ps, heads, cs, sn, ra, rb, dst, dst_ap):
            hf = AD // 2
            xv = ps[:, 0:heads * AD].rearrange("p (h d) -> p h d", h=heads)
            av = ra[:, 0:heads * AD].rearrange("p (h d) -> p h d", h=heads)
            bv = rb[:, 0:heads * AD].rearrange("p (h d) -> p h d", h=heads)
            wait("DVE", ps.full)
            wait("DVE", tab.full)
            wait("DVE", ra.free)
            wait("DVE", rb.free)
            done("DVE", V.tensor_tensor(av, xv, cs.unsqueeze(1).to_broadcast([P, heads, AD]), ALU.mult), ra.full)
            for d0, s0 in ((0, hf), (hf, 0)):
                m = done("DVE", V.tensor_tensor(bv[:, :, d0:d0 + hf], xv[:, :, s0:s0 + hf],
                                              sn[:, d0:d0 + hf].unsqueeze(1).to_broadcast([P, heads, hf]), ALU.mult), rb.full, ps.free)
            wait("POOL", ra.full)
            wait("POOL", rb.full)
            done("POOL", G.tensor_tensor(dst_ap.rearrange("p (h c d) -> p h c d", h=heads, c=2),
                                       av.unsqueeze(2).to_broadcast([P, heads, 2, AD]),
                                       bv.unsqueeze(2).to_broadcast([P, heads, 2, AD]), ALU.add), dst.full, ra.free, rb.free)

        with ExitStack() as xs:
            xsb = lambda n, s, d=F32: sb(n, s, d, xs)
            g_lo = xsb("g_lo", [P, H * KVC])
            g_hi = xsb("g_hi", [P, H * KVC])
            vo = xsb("vo", [P, H * D])
            wqr_lo = xsb("wqr_lo", [P, H * R])
            wqr_hi = xsb("wqr_hi", [P, H * R])
            wdq = xsb("wdq", [P, DC * QC])
            wkvc = xsb("wkvc", [P, DC * KVC])
            wkr = xsb("wkr", [P, 2 * R])
            cg = xsb("cg", [P, WIN * D])
            rt = xsb("rt", [P, WIN * 2 * R])
            segi = xsb("segi", [P, NT], I32)
            seg = xsb("seg", [P, NT + 1])
            beg = xsb("beg", [P, NT + 1])
            upos = xsb("upos", [P, NT])
            idxc = xsb("idxc", [P, 1], I32)
            idxr = xsb("idxr", [P, 1], I32)
            bstart = xsb("bstart", [P, NT + 1])
            pat = xsb("pat", [P, 2 * GK])
            msk = xsb("msk", [P, GN], BF16)
            mtmp = xsb("mtmp", [P, 2 * GK])
            eg = xsb("eg", [P, NG * P], BF16)

            load(segi, segi[:], a["itok"].rearrange("b (t p) -> p (b t)", p=P))
            load(bstart, bstart[:], a["bstart"])
            load(pat, pat[:], a["pat"])
            load(wdq, wdq[:].rearrange("p (k n) -> p k n", k=DC), a["W_dq"].rearrange("(k p) n -> p k n", p=P))

            wait("DVE", segi.full)
            wait("DVE", bstart.full)
            done("DVE", V.tensor_copy(seg[:, 0:NT], segi[:]), seg.full)
            wait("DVE", seg.full)
            done("DVE", V.tensor_copy(seg[:, NT:NT + 1], seg[:, 0:1]), seg.full)
            wait("DVE", seg.full)
            done("DVE", V.tensor_scalar(beg[:], seg[:], -float(LOOKBACK), 0.0, ALU.add, ALU.max), beg.full)
            wait("DVE", beg.full)
            done("DVE", V.tensor_scalar(beg[:], beg[:], float(LK - WIN), None, ALU.min), beg.full)
            wait("DVE", beg.full)
            done("DVE", V.tensor_tensor(upos[:], seg[:, 0:NT], beg[:, 0:NT], ALU.subtract), upos.full)

            def gather(t):
                wait("DVE", beg.full)
                wait("DVE", idxc.free)
                wait("DVE", idxr.free)
                done("DVE", V.tensor_tensor(idxc[:], beg[:, bass.ds(t, 1)], bstart[:, bass.ds(t, 1)], ALU.add), idxc.full)
                done("DVE", V.tensor_copy(idxr[:], beg[:, bass.ds(t, 1)]), idxr.full)
                for buf, idx, src in ((cg, idxc, a["ctx"].rearrange("b s d -> (b s) d")), (rt, idxr, a["ktab"])):
                    ln = dma_line(buf, software=True)
                    wait("POOL", buf.free)
                    wait("POOL", idx.full)
                    c.hold("POOL")
                    done(ln, G.indirect_dma_start(buf[:], None, src, bass.IndirectOffsetOnAxis(ap=idx[:, 0:1], axis=0)),
                         buf.full, idx.free)

            gather(0)

            load(tab, tab[:].rearrange("p (t d) -> p t d", t=NT), a["qtab"].rearrange("(t p) d -> p t d", p=P))
            load(wkvc, wkvc[:].rearrange("p (k n) -> p k n", k=DC), a["W_kvc"].rearrange("(k p) n -> p k n", p=P))
            load(wkr, wkr[:, 0:R], a["W_kr"])
            load(wkr, wkr[:, R:R + R // 2], a["W_kr"][:, R // 2:R])
            load(wkr, wkr[:, R + R // 2:2 * R], a["W_kr"][:, 0:R // 2])
            load(wqr_lo, wqr_lo[:], a["W_qr"][0:QLO, :])
            done("POOL", G.memset(wqr_hi[:], 0.0), wqr_hi.full)
            wait("SP", wqr_hi.full)
            load(wqr_hi, wqr_hi[0:QHI, :], a["W_qr"][QLO:QC, :])
            done("POOL", G.memset(g_hi[:], 0.0), g_hi.full)
            done("POOL", G.memset(msk[:], 0.0), msk.full)
            wait("DVE", ident.full)
            done("DVE", V.tensor_copy(eg[:].rearrange("p (q h) -> p q h", h=H),
                                    ident[:].unsqueeze(2).to_broadcast([P, P, H])), eg.full)

            with ExitStack() as hs:
                HU = 4
                sets = [dict(uq_lo=sb(f"uq_lo{s}", [P, HD], F32, hs), uq_hi=sb(f"uq_hi{s}", [QHI, HD], F32, hs),
                             uk=sb(f"uk{s}", [KVC, HD], F32, hs), uv=sb(f"uv{s}", [KVC, HD], F32, hs),
                             wo=sb(f"wo{s}", [HD, D], F32, hs)) for s in range(HU)]
                tw = Ring([sb(f"tw{i}", [P, 2 * P + QC], F32, hs) for i in range(2)])
                wait("DVE", g_hi.full)
                for w in sets:
                    for buf in w.values():
                        dma_line(buf)
                with c.loop("heads", H // HU) as hi:
                    for s in range(HU):
                        w = sets[s]
                        col = hi * (HU * HD) + s * HD
                        for k, src in (("uq_lo", a["W_uq"][0:QLO, bass.ds(col, HD)]),
                                       ("uq_hi", a["W_uq"][QLO:QC, bass.ds(col, HD)]),
                                       ("uk", a["W_uk"][:, bass.ds(col, HD)]),
                                       ("uv", a["W_uv"][:, bass.ds(col, HD)]),
                                       ("wo", a["W_o"][bass.ds(col, HD), :])):
                            wait("SP", w[k].free)
                            load(w[k], w[k][:], src)
                        ps = banks.take()
                        wait("PE", ps.free)
                        for k, o, n in (("uq_lo", 0, P), ("uq_hi", P, QHI), ("uk", QC, P), ("uv", QC + P, P)):
                            wait("PE", w[k].full)
                            c.hold("PE")
                            m = done("PE", T.transpose(ps[:, o:o + n], w[k][:], ident[0:n, 0:n]), ps.full, w[k].free)
                        t = tw.take()
                        wait("ACT", t.free)
                        evac(t, t[:], ps, ps[:, 0:2 * P + QC], "ACT")
                        wait("PE", t.full)
                        pg = banks.take()
                        wait("PE", pg.free)
                        matmuls([(pg[:, 0:P], [(t[:, 0:P], t[:, QC:QC + P])]),
                                     (pg[0:QHI, P:2 * P], [(t[:, P:QC], t[:, QC:QC + P])])], pg.full, t.free)
                        evac(g_lo, g_lo[:, bass.ds(col, P)], pg, pg[:, 0:P], "DVE")
                        evac(g_hi, g_hi[0:QHI, bass.ds(col, P)], pg, pg[0:QHI, P:2 * P], "DVE")
                        pv = banks.take()
                        wait("PE", pv.free)
                        wait("PE", w["wo"].full)
                        matmuls([(pv[:], [(t[:, QC + P:QC + 2 * P], w["wo"][:])])], pv.full, t.free, w["wo"].free)
                        evac(vo, vo[:, bass.ds(hi * (HU * D) + s * D, D)], pv, pv[:], ("ACT", "DVE")[s % 2])

            for e in ("PE", "ACT", "DVE", "POOL", "SP"):
                for o in ("PE", "ACT", "DVE"):
                    c.wait_mark(e, Mark(c.lines[o], c.lines[o].n, ()))
            load(wq, wq[:].rearrange("p (k n) -> p k n", k=DC), a["Wq"].rearrange("(k p) n -> p k n", p=P))

            qc = xsb("qc", [P, 2 * P])
            ct = Ring([xsb(f"ct{i}", [P, DC * 3 * P]) for i in range(2)])
            kc = xsb("kc", [P, NG * GK + GN - GK])
            kr = xsb("kr", [P, NG * GK + GN - GK])
            rtT = xsb("rtT", [P, WIN * P])
            kn = xsb("kn", [P, NG * KVC])
            pt = Ring([xsb(f"pt{i}", [P, 4 * P]) for i in range(2)])
            pr = Ring([xsb(f"pr{i}", [P, 4 * GK]) for i in range(2)])
            sm = Ring([xsb(f"sm{i}", [P, 12]) for i in range(2)])
            qa = xsb("qa", [P, P * H])
            qr = xsb("qr", [P, P * H])
            qn = xsb("qn", [P, H * 2 * R])
            oc = xsb("oc", [P, P * H])
            ra, rb = xsb("ra", [P, 512]), xsb("rb", [P, 512])
            done("POOL", G.memset(qc[:], 0.0), qc.full)
            done("POOL", G.memset(kn[:], 0.0), kn.full)
            for b_ in pt.bufs:
                done("POOL", G.memset(b_[:], 0.0), b_.full)
            for b_ in (kc, kr):
                zeroed = done("POOL", G.memset(b_[:, NG * GK:], 0.0), b_.full)
            for e in ("PE", "ACT", "DVE"):
                c.wait_mark(e, zeroed)

            def by_hq(buf, h0, n):
                return buf[:].rearrange("p (q h) -> p h q", h=H)[:, h0:h0 + n, :]

            with c.loop("tiles", NT) as ti:
                xin = x1[:, bass.ds(ti * D, D)]
                layer_norm(xin)
                transpose_h()

                wait("DVE", mtmp.free)
                wait("DVE", msk.free)
                uc = upos[:, bass.ds(ti, 1)]
                done("DVE", V.tensor_scalar(mtmp[:, 0:GK], pat[:, GK:], uc, NEG, ALU.is_gt, ALU.mult), mtmp.full)
                done("DVE", V.tensor_scalar(mtmp[:, GK:], pat[:, GK:], uc, -float(LOOKBACK), ALU.subtract, ALU.is_lt), mtmp.full)
                wait("DVE", mtmp.full)
                m1 = done("DVE", V.scalar_tensor_tensor(mtmp[:, GK:], mtmp[:, GK:], NEG, mtmp[:, 0:GK], ALU.mult, ALU.add), mtmp.full)
                wait("DVE", mtmp.full)
                done("DVE", V.tensor_tensor(msk[:, 0:GK], mtmp[:, GK:], pat[:, 0:GK], ALU.add), msk.full, mtmp.free)

                wait("PE", cg.full)
                wait("ACT DVE", kc.free)
                for s in range(WIN // 3):
                    cb = ct.take()
                    wait("ACT DVE", cb.free)
                    for jj in range(3):
                        ps = banks.take()
                        wait("PE", ps.free)
                        for k in range(DC):
                            o = (3 * s + jj) * D + k * P
                            ins = T.transpose(ps[:, k * P:(k + 1) * P], cg[:, o:o + P], ident[:])
                        done("PE", ins, ps.full, cg.free)
                        evac(cb, cb[:].rearrange("p (k j q) -> p k j q", k=DC, j=3)[:, :, jj, :], ps,
                             ps[:].rearrange("p (k q) -> p k q", k=DC))
                    ps = banks.take()
                    wait("PE", ps.free)
                    wait("PE", cb.full)
                    wait("PE", wkvc.full)
                    matmuls([(ps[:, 0:3 * P], [(wkvc[:, k * KVC:(k + 1) * KVC], cb[:, k * 3 * P:(k + 1) * 3 * P])
                                                   for k in range(DC)])], ps.full, cb.free)
                    src = ps[:, 0:3 * P].rearrange("p (j g q) -> p j g q", j=3, g=NG)
                    dst = kc[:, 0:NG * GK].rearrange("p (g j q) -> p j g q", g=NG, j=WIN)[:, 3 * s:3 * s + 3]
                    evac(kc, dst, ps, src, "DVE")

                wait("PE", rt.full)
                wait("ACT DVE", rtT.free)
                for s in range(WIN // 3):
                    ps = banks.take()
                    wait("PE", ps.free)
                    for jj in range(3):
                        ins = T.transpose(ps[:, jj * P:(jj + 1) * P], rt[:, (3 * s + jj) * P:(3 * s + jj + 1) * P], ident[:])
                    done("PE", ins, ps.full, rt.free)
                    evac(rtT, rtT[:].rearrange("p (g j q) -> p j g q", g=NG, j=WIN)[:, 3 * s:3 * s + 3], ps,
                         ps[:, 0:3 * P].rearrange("p (j g q) -> p j g q", j=3, g=NG))

                gather(ti + 1)

                pq = banks.take()
                wait("PE", pq.free)
                wait("PE", hT.full)
                wait("PE", wdq.full)
                matmuls([(pq[:, 0:P], [(wdq[:, k * QC:k * QC + QLO], hT[:, k * P:(k + 1) * P]) for k in range(DC)]),
                             (pq[0:QHI, P:2 * P], [(wdq[:, k * QC + QLO:(k + 1) * QC], hT[:, k * P:(k + 1) * P])
                                                   for k in range(DC)])], pq.full, hT.free)
                wait("ACT", qc.free)
                evac(qc, qc[:, 0:P], pq, pq[:, 0:P], "ACT")
                evac(qc, qc[0:QHI, P:2 * P], pq, pq[0:QHI, P:2 * P], "ACT")

                wait("PE", qc.full)
                wait("PE", wqr_lo.full)
                wait("PE", wqr_hi.full)
                wait("POOL", qn.free)
                tb = tab[:, bass.ds(ti * P, P)]
                for n in range(2):
                    ps = banks.take()
                    wait("PE", ps.free)
                    matmuls([(ps[:], [(qc[:, 0:P], wqr_lo[:, n * 512:(n + 1) * 512]),
                                          (qc[:, P:2 * P], wqr_hi[:, n * 512:(n + 1) * 512])])], ps.full, qc.free)
                    rope(ps, 8, tab[:, bass.ds(ti * P, AD)], tab[:, bass.ds(ti * P + AD, AD)], ra, rb,
                         qn, qn[:, n * 1024:(n + 1) * 1024])

                wait("ACT DVE", qa.free)
                for n in range(4):
                    ps = banks.take()
                    wait("PE", ps.free)
                    matmuls([(ps[:, i * P:(i + 1) * P],
                                  [(g_lo[:, h * P:(h + 1) * P], qc[:, 0:P]), (g_hi[:, h * P:(h + 1) * P], qc[:, P:2 * P])])
                                 for i, h in enumerate(range(4 * n, 4 * n + 4))], ps.full, qc.free)
                    evac(qa, by_hq(qa, 4 * n, 4), ps, ps[:].rearrange("p (h q) -> p h q", h=4))

                wait("DVE", rtT.full)
                wait("PE", kc.full)
                wait("PE", wkr.full)
                wait("DVE", kr.free)
                for s in range(WIN // 3):
                    ps = banks.take()
                    wait("PE", ps.free)
                    matmuls([(ps[:, 0:3 * P], [(wkr[:], kc[:, s * 3 * P:(s + 1) * 3 * P])])], ps.full, kc.free)
                    wait("DVE", ps.full)
                    done("DVE", V.tensor_tensor(kr[:, s * 3 * P:(s + 1) * 3 * P], ps[:, 0:3 * P],
                                              rtT[:, s * 3 * P:(s + 1) * 3 * P], ALU.mult), kr.full, ps.free, rtT.free)

                wait("ACT DVE", qr.free)
                wait("PE", qn.full)
                for n in range(4):
                    ps = banks.take()
                    wait("PE", ps.free)
                    for i in range(4):
                        ins = T.transpose(ps[:, i * P:(i + 1) * P], qn[:, (4 * n + i) * P:(4 * n + i + 1) * P], ident[:])
                    done("PE", ins, ps.full, qn.free)
                    evac(qr, by_hq(qr, 4 * n, 4), ps, ps[:].rearrange("p (h q) -> p h q", h=4))

                wait("PE", qa.full)
                wait("PE", qr.full)
                wait("PE", kr.full)
                wait("PE", msk.full)
                wait("PE", eg.full)

                def scores(n):
                    ps = banks.take()
                    wait("PE", ps.free)
                    matmuls([(ps[:, i * GN:(i + 1) * GN],
                                  [(eg[:, g * P:(g + 1) * P], msk[:]),
                                   (qa[:, g * P:(g + 1) * P], kc[:, g * GK:g * GK + GN]),
                                   (qr[:, g * P:(g + 1) * P], kr[:, g * GK:g * GK + GN])])
                                 for i, g in enumerate(range(4 * n, 4 * n + 4))], ps.full, qa.free, qr.free, kc.free, kr.free, msk.free)
                    p, s = pr.take(), sm.take()
                    sv = ps[:, 0:4 * GN].rearrange("p (g k) -> p g k", g=4)[:, :, 0:GK]
                    pv = p[:].rearrange("p (g k) -> p g k", g=4)
                    wait("DVE", ps.full)
                    wait("DVE", s.free)
                    wait("DVE", p.free)
                    done("DVE", V.tensor_reduce(s[:, 0:4], sv, AX.X, ALU.max), s.full)
                    wait("DVE", s.full)
                    done("DVE", V.tensor_tensor(pv, sv, s[:, 0:4].unsqueeze(2).to_broadcast([P, 4, GK]), ALU.subtract), p.full, ps.free)
                    wait("ACT", p.full)
                    done("ACT", A.activation(p[:], p[:], ACT.Exp, scale=XSCALE), p.full)
                    wait("DVE", p.full)
                    done("DVE", V.tensor_reduce(s[:, 4:8], pv, AX.X, ALU.add), s.full)
                    wait("DVE", s.full)
                    done("DVE", V.reciprocal(s[:, 8:12], s[:, 4:8]), s.full)
                    wait("POOL", s.full)
                    wait("POOL", p.full)
                    done("POOL", G.tensor_tensor(pv, pv, s[:, 8:12].unsqueeze(2).to_broadcast([P, 4, GK]), ALU.mult), p.full, s.free)
                    return p

                def values(n, p):
                    ps = banks.take()
                    wait("PE", ps.free)
                    wait("PE", p.full)
                    for i in range(4):
                        ins = T.transpose(ps[0:GK, i * P:(i + 1) * P], p[:, i * GK:(i + 1) * GK], ident[:])
                    done("PE", ins, ps.full, p.free)
                    q = pt.take()
                    wait("ACT", q.free)
                    evac(q, q[0:GK, :], ps, ps[0:GK, :], "ACT")
                    ps = banks.take()
                    wait("PE", ps.free)
                    wait("PE", q.full)
                    matmuls([(ps[:, i * P:(i + 1) * P], [(kn[:, (4 * n + i) * P:(4 * n + i + 1) * P],
                                                              q[:, i * P:(i + 1) * P])]) for i in range(4)], ps.full, q.free, kn.free)
                    evac(oc, oc[:, n * 512:(n + 1) * 512], ps, ps[:])

                def key_rows(n):
                    ps = banks.take()
                    wait("PE", ps.free)
                    for i in range(4):
                        g = 4 * n + i
                        ins = T.transpose(ps[0:GK, i * P:(i + 1) * P], kc[:, g * GK:(g + 1) * GK], ident[:])
                    done("PE", ins, ps.full, kc.free)
                    evac(kn, kn[0:GK, n * 512:(n + 1) * 512], ps, ps[0:GK, :])

                wait("ACT DVE", oc.free)
                wait("ACT DVE", kn.free)
                p0 = scores(0)
                key_rows(0)
                p1 = scores(1)
                key_rows(1)
                key_rows(2)
                wait("PE", kn.full)
                values(0, p0)
                p2 = scores(2)
                key_rows(3)
                wait("PE", kn.full)
                values(1, p1)
                p3 = scores(3)
                values(2, p2)
                values(3, p3)

                wait("PE", psO.free)
                wait("PE", oc.full)
                wait("PE", vo.full)
                ov = oc[:].rearrange("p (q h) -> p h q", h=H)
                matmuls([(psO[:], [(ov[:, h, :], vo[:, h * D:(h + 1) * D]) for h in range(H)])], psO.full, oc.free)
                wait("DVE", psO.full)
                done("DVE", V.tensor_tensor(xin, psO[:], xin, ALU.add), x1.full, psO.free)

        for e in ("PE", "ACT", "DVE", "POOL", "SP"):
            for o in ("PE", "ACT", "DVE", "POOL", "d_cg", "d_rt"):
                c.wait_mark(e, Mark(c.lines[o], c.lines[o].n, ()))

        qwg = sb("qwg", [P, DC * FI], BF16)
        qwu = sb("qwu", [P, DC * FI], BF16)
        qwd = sb("qwd", [P, NFC * D], BF16)
        wsg = sb("wsg", [P, FI])
        wsu = sb("wsu", [P, FI])
        wsd = sb("wsd", [P, D])
        identb = sb("identb", [P, P], BF16)
        ones = sb("ones", [P, P])
        yq, mq = sb("yq", [P, FI]), sb("mq", [P, FI])
        qs = sb("qs", [P, 4])
        done("DVE", V.tensor_copy(identb[:], ident[:]), identb.full)
        done("POOL", G.memset(ones[:], 1.0), ones.full)
        zeroed = done("POOL", G.memset(qwd[:], 0.0), qwd.full)

        def quantise(src, src_ap, n, rows, dst, dst_ap, *gates):
            wait("DVE", src.full)
            wait("DVE", qs.free)
            done("DVE", V.tensor_reduce(qs[0:rows, 0:1], src_ap, AX.X, ALU.max, apply_absolute_value=True), qs.full)
            wait("DVE", qs.full)
            done("DVE", V.reciprocal(qs[0:rows, 1:2], qs[0:rows, 0:1]), qs.full)
            wait("DVE", qs.full)
            done("DVE", V.tensor_scalar(qs[0:rows, 3:4], qs[0:rows, 1:2], FP8_MAX, None, ALU.mult), qs.full)
            done("DVE", V.tensor_scalar(qs[0:rows, 2:3], qs[0:rows, 0:1], 1.0 / FP8_MAX, None, ALU.mult), qs.full)
            y, m = yq[0:rows, 0:n], mq[0:rows, 0:n]
            wait("ACT", yq.free)
            wait("DVE", mq.free)
            wait("ACT", src.full)
            wait("ACT", qs.full)
            done("ACT", A.activation(y, src_ap, ACT.Copy, scale=qs[0:rows, 3:4]), yq.full, src.free, qs.free)
            wait("DVE", yq.full)
            done("DVE", V.tensor_scalar(m.bitcast(U32), y.bitcast(U32), 0x7F800000, 0x00400000,
                                      ALU.bitwise_and, ALU.bitwise_or), mq.full)
            wait("DVE", mq.full)
            done("DVE", V.tensor_scalar(m, m, 1.5 * 2.0 ** -6, 2.0 ** 20, ALU.max, ALU.mult), mq.full)
            wait("POOL", mq.full)
            wait("POOL", yq.full)
            done("POOL", G.tensor_tensor(y, y, m, ALU.add), yq.full)
            wait("DVE", yq.full)
            wait("DVE", dst.free)
            return done("DVE", V.tensor_tensor(dst_ap, y, m, ALU.subtract), dst.full, yq.free, mq.free, *gates)

        def spread(scale_ap, rows, dst, dst_ap):
            wait("DVE", dg.free)
            wait("DVE", ident.full)
            done("DVE", V.tensor_scalar(dg[0:rows, 0:rows], ident[0:rows, 0:rows], scale_ap, None, ALU.mult), dg.full, qs.free)
            ps = banks.take()
            wait("PE", ps.free)
            wait("PE", dg.full)
            wait("PE", ones.full)
            matmuls([(ps[:, 0:rows], [(ones[0:rows, :], dg[0:rows, 0:rows])])], ps.full, dg.free)
            evac(dst, dst_ap, ps, ps[:, 0:rows])

        with ExitStack() as ss:
            ssb = lambda n, s, d=F32: sb(n, s, d, ss)
            wk, wv = ssb("wk", [P, DC * NKV * AD]), ssb("wv", [P, DC * NKV * AD])
            wao = ssb("wao", [P, 8 * D])
            sn = ssb("sn", [P, NH * 2 * AD])
            kn2 = ssb("kn2", [P, NKV * P])
            sa, sbb = ssb("sa", [P, 512]), ssb("sbb", [P, 512])
            qT = ssb("qT", [P, NH * S])
            kT = ssb("kT", [P, NKV * S])
            v1 = ssb("v1", [P, TPB * NKV * VW])
            px = Ring([ssb(f"px{i}", [P, 3 * REP * P]) for i in range(2)])
            tri = ssb("tri", [P, P])
            rden = Ring([ssb(f"rden{i}", [P, 2 * REP]) for i in range(2)])
            yn = ssb("yn", [P, TPB * NH * AD])
            yT = ssb("yT", [P, NH * AD])
            wr = Ring([ssb(f"wr{i}", [P, D]) for i in range(2)])
            wdr = ssb("wdr", [P, FI])
            di = Ring([ssb(f"di{i}", [P, 1], I32) for i in range(3)])
            wb = ssb("wb", [P, FI], BF16)
            dg = ssb("dg", [P, P])
            for buf in (*di.bufs, wdr):
                dma_line(buf)
            for buf in wr.bufs:
                dma_line(buf, software=True)
            load(wk, wk[:].rearrange("p (k n) -> p k n", k=DC), a["Wk"].rearrange("(k p) n -> p k n", p=P))
            load(wv, wv[:].rearrange("p (k n) -> p k n", k=DC), a["Wv"].rearrange("(k p) n -> p k n", p=P))
            load(wao, wao[:].rearrange("p (k n) -> p k n", k=8), a["Wo"].rearrange("(k p) n -> p k n", p=P))
            load(tri, tri[:], a["tri"])
            v1v = v1[:].rearrange("p (x w) -> p x w", w=VW)
            done("DVE", V.memset(v1v[:, :, AD:AD + 1], 1.0), v1.full)
            vz = done("DVE", V.memset(v1v[:, :, AD + 1:], 0.0), v1.full)
            for e in ("PE", "ACT", "DVE"):
                c.wait_mark(e, vz)
                c.wait_mark(e, zeroed)

            def quantise_weights(ti):
                for s, (o, n) in enumerate(FCH):
                    d = di.take()
                    wait("SP", d.free)
                    load(d, d[0:n, :], a["d_idx"].rearrange("(n o) -> n o", o=1)[bass.ds(ti * FT + o, n), :])
                    for src, qw, ws in ((a["w_gate"], qwg, wsg), (a["w_up"], qwu, wsu)):
                        w = wr.take()
                        ln = dma_line(w)
                        wait("POOL", w.free)
                        wait("POOL", d.full)
                        c.hold("POOL")
                        done(ln, G.indirect_dma_start(w[0:n, :], None, src,
                                                      bass.IndirectOffsetOnAxis(ap=d[0:n, 0:1], axis=0)), w.full)
                        quantise(w, w[0:n, :], D, n, wb, wb[0:n, 0:D], d.free)
                        spread(qs[0:n, 2:3], n, ws, ws[:, bass.ds(ti * FT + o, n)])
                        ps = banks.take()
                        wait("PE", ps.free)
                        wait("PE", wb.full)
                        wait("PE", identb.full)
                        pb = ps[:].bitcast(BF16)
                        for k in range(DC):
                            ins = T.transpose(pb[:, k * P:k * P + n], wb[0:n, k * P:(k + 1) * P], identb[0:n, 0:n])
                        done("PE", ins, ps.full, wb.free)
                        evac(qw, qw[:].rearrange("p (k m) -> p k m", k=DC)[:, :, bass.ds(ti * FT + o, n)], ps,
                             pb[:, 0:DC * P].rearrange("p (k m) -> p k m", k=DC)[:, :, 0:n], "ACT")
                wait("SP", wdr.free)
                load(wdr, wdr[:], a["w_down"][bass.ds(ti * P, P), :])
                quantise(wdr, wdr[:], FI, P, wb, wb[:])
                spread(qs[:, 2:3], P, wsd, wsd[:, bass.ds(ti * P, P)])
                for i in range(NT):
                    ps = banks.take()
                    wait("PE", ps.free)
                    wait("PE", wb.full)
                    pb = ps[:].bitcast(BF16)
                    for s, (o, n) in enumerate(FCH):
                        ins = T.transpose(pb[0:n, s * P:(s + 1) * P], wb[:, i * FT + o:i * FT + o + n], identb[:])
                    done("PE", ins, ps.full, wb.free)
                    qv = qwd[:].rearrange("p (c o) -> p c o", o=D)
                    pv = pb[:, 0:3 * P].rearrange("p (s o) -> p s o", s=3)
                    evac(qwd, qv[:, 3 * i:3 * i + 2, bass.ds(ti * P, P)], ps, pv[:, 0:2, :], "ACT")
                    evac(qwd, qv[0:FCH[2][1], 3 * i + 2, bass.ds(ti * P, P)], ps, pv[0:FCH[2][1], 2, :], "ACT")

            with c.loop("batches", B) as b:
                wait("ACT DVE", qT.free)
                wait("ACT DVE", kT.free)
                wait("ACT DVE", v1.free)
                with c.loop("btiles", TPB) as t:
                    ti = b * TPB + t
                    xin = x1[:, bass.ds(ti * D, D)]
                    layer_norm(xin)
                    transpose_h()
                    wait("PE", hT.full)
                    for w in (wq, wk, wv):
                        wait("PE", w.full)
                    cos, sin = tab[:, bass.ds(ti * P, AD)], tab[:, bass.ds(ti * P + AD, AD)]
                    wait("POOL", sn.free)
                    for n in range(2):
                        ps = banks.take()
                        wait("PE", ps.free)
                        matmuls([(ps[:], [(hT[:, k * P:(k + 1) * P], wq[:, k * 1024 + n * 512:k * 1024 + (n + 1) * 512])
                                              for k in range(DC)])], ps.full, hT.free)
                        rope(ps, 8, cos, sin, sa, sbb, sn, sn[:, n * 1024:(n + 1) * 1024])
                    ps = banks.take()
                    wait("PE", ps.free)
                    matmuls([(ps[:], [(hT[:, k * P:(k + 1) * P], wk[:, k * 512:(k + 1) * 512]) for k in range(DC)])], ps.full, hT.free)
                    wait("DVE", ps.full)
                    wait("DVE", kn2.free)
                    kv = ps[:].rearrange("p (h d) -> p h d", h=NKV)
                    ko = kn2[:].rearrange("p (h d) -> p h d", h=NKV)
                    done("DVE", V.tensor_tensor(ko[:, :, 0:AD], kv, cos.unsqueeze(1).to_broadcast([P, NKV, AD]), ALU.mult), kn2.full)
                    for d0, s0 in ((0, AD // 2), (AD // 2, 0)):
                        done("DVE", V.tensor_tensor(ko[:, :, AD + d0:AD + d0 + AD // 2], kv[:, :, s0:s0 + AD // 2],
                                                  sin[:, d0:d0 + AD // 2].unsqueeze(1).to_broadcast([P, NKV, AD // 2]), ALU.mult), kn2.full, ps.free)
                    ps = banks.take()
                    wait("PE", ps.free)
                    matmuls([(ps[:], [(hT[:, k * P:(k + 1) * P], wv[:, k * 512:(k + 1) * 512]) for k in range(DC)])], ps.full, hT.free)
                    evac(v1, v1[:, bass.ds(t * (NKV * VW), NKV * VW)].rearrange("p (h w) -> p h w", w=VW)[:, :, 0:AD], ps,
                         ps[:].rearrange("p (h d) -> p h d", h=NKV), "ACT")
                    wait("PE", kn2.full)
                    for n in range(2):
                        ps = banks.take()
                        wait("PE", ps.free)
                        for i in range(4):
                            ins = T.transpose(ps[:, i * P:(i + 1) * P], kn2[:, (4 * n + i) * P:(4 * n + i + 1) * P], ident[:])
                        done("PE", ins, ps.full, kn2.free)
                        evac(kT, kT[:].rearrange("p (h s) -> p h s", s=S)[:, 4 * n:4 * n + 4, bass.ds(t * P, P)], ps,
                             ps[:].rearrange("p (h q) -> p h q", h=4))
                    wait("PE", sn.full)
                    for n in range(4):
                        ps = banks.take()
                        wait("PE", ps.free)
                        for i in range(4):
                            ins = T.transpose(ps[:, i * P:(i + 1) * P], sn[:, (4 * n + i) * P:(4 * n + i + 1) * P], ident[:])
                        done("PE", ins, ps.full, sn.free)
                        evac(qT, qT[:].rearrange("p (h s) -> p h s", s=S)[:, 4 * n:4 * n + 4, bass.ds(t * P, P)], ps,
                             ps[:].rearrange("p (h q) -> p h q", h=4))
                    quantise_weights(ti)

                wait("PE", qT.full)
                wait("PE", kT.full)
                wait("PE", v1.full)
                wait("DVE", yn.free)

                def att_scores(kh):
                    q3 = qT[:, kh * REP * S:(kh + 1) * REP * S].rearrange("p (r q) -> p r q", r=REP)
                    p0 = banks.take()
                    wait("PE", p0.free)
                    matmuls([(p0[:], [(kT[:, kh * S:kh * S + P], qT[:, kh * REP * S:(kh + 1) * REP * S])])], p0.full, kT.free, qT.free)
                    p1 = banks.take()
                    wait("PE", p1.free)
                    matmuls([(p1[:, 0:REP * P], [(kT[:, kh * S + P:(kh + 1) * S], q3[:, :, P:S])])], p1.full, kT.free, qT.free)
                    x = px.take()
                    wait("ACT", x.free)
                    wait("ACT", p0.full)
                    done("ACT", A.activation(x[:, 0:REP * S], p0[:], ACT.Tanh, scale=ASCALE / SOFTCAP), x.full, p0.free)
                    wait("ACT", p1.full)
                    done("ACT", A.activation(x[:, REP * S:], p1[:, 0:REP * P], ACT.Tanh, scale=ASCALE / SOFTCAP), x.full, p1.free)
                    wait("ACT", x.full)
                    done("ACT", A.activation(x[:], x[:], ACT.Exp, scale=SOFTCAP), x.full)
                    wait("POOL", x.full)
                    wait("POOL", tri.full)
                    d0 = x[:, 0:REP * S].rearrange("p (r q) -> p r q", r=REP)[:, :, 0:P]
                    d1 = x[:, REP * S:].rearrange("p (r q) -> p r q", r=REP)
                    for d in (d0, d1):
                        done("POOL", G.tensor_tensor(d, d, tri[:].unsqueeze(1).to_broadcast([P, REP, P]), ALU.mult), x.full)
                    return x

                def att_values(kh, x):
                    y = banks.take()
                    wait("PE", y.free)
                    wait("PE", x.full)
                    va, vb = v1[:, kh * VW:(kh + 1) * VW], v1[:, (NKV + kh) * VW:(NKV + kh + 1) * VW]
                    parts = [(y[:, r * VW:(r + 1) * VW], [(x[:, r * S:r * S + P], va)]) for r in range(REP)]
                    parts += [(y[:, (REP + r) * VW:(REP + r + 1) * VW],
                               [(x[:, r * S + P:(r + 1) * S], va), (x[:, REP * S + r * P:REP * S + (r + 1) * P], vb)])
                              for r in range(REP)]
                    matmuls(parts, y.full, x.free, v1.free)
                    rd = rden.take()
                    wait("DVE", y.full)
                    wait("DVE", rd.free)
                    yv = y[:, 0:2 * REP * VW].rearrange("p (t r w) -> p t r w", t=TPB, w=VW)
                    done("DVE", V.reciprocal(rd[:], y[:, AD:AD + (2 * REP - 1) * VW + 1:VW]), rd.full)
                    wait("DVE", rd.full)
                    done("DVE", V.tensor_tensor(
                        yn[:].rearrange("p (t r w) -> p t r w", t=TPB, w=AD)[:, :, kh * REP:(kh + 1) * REP, :], yv[:, :, :, 0:AD],
                        rd[:].rearrange("p (t r) -> p t r", t=TPB).unsqueeze(3).to_broadcast([P, TPB, REP, AD]), ALU.mult), yn.full, y.free, rd.free)

                x_prev = att_scores(0)
                for kh in range(NKV):
                    x_next = att_scores(kh + 1) if kh + 1 < NKV else None
                    att_values(kh, x_prev)
                    x_prev = x_next

                wait("PE", yn.full)
                wait("PE", wao.full)
                for qt in range(TPB):
                    wait("ACT DVE", yT.free)
                    for n in range(2):
                        ps = banks.take()
                        wait("PE", ps.free)
                        for i in range(4):
                            o = qt * NH * AD + (4 * n + i) * P
                            ins = T.transpose(ps[:, i * P:(i + 1) * P], yn[:, o:o + P], ident[:])
                        done("PE", ins, ps.full, yn.free)
                        evac(yT, yT[:, n * 512:(n + 1) * 512], ps, ps[:])
                    wait("PE", psO.free)
                    wait("PE", yT.full)
                    matmuls([(psO[:], [(yT[:, k * P:(k + 1) * P], wao[:, k * D:(k + 1) * D]) for k in range(8)])], psO.full, yT.free)
                    xo = x1[:, bass.ds(b * (TPB * D) + qt * D, D)]
                    wait("DVE", psO.full)
                    done("DVE", V.tensor_tensor(xo, psO[:], xo, ALU.add), x1.full, psO.free)

        for e in ("PE", "ACT", "DVE", "POOL", "SP"):
            for o in ("PE", "ACT", "DVE", "POOL"):
                c.wait_mark(e, Mark(c.lines[o], c.lines[o].n, ()))

        xq = sb("xq", [P, D], BF16)
        xqT = sb("xqT", [P, D], BF16)
        gb, ub = sb("gb", [P, FI]), sb("ub", [P, FI])
        tq = sb("tq", [P, FI], BF16)
        tqT = sb("tqT", [P, NFC * P], BF16)
        sx = sb("sx", [P, 2])
        ot = sb("ot", [P, D])
        c.line("d_out", 16)
        zeroed = done("POOL", G.memset(tqT[:], 0.0), tqT.full)
        for e in ("ACT", "DVE"):
            c.wait_mark(e, zeroed)
        wait("DVE", x1.full)
        with c.loop("ffn", NT) as ti:
            xin = x1[:, bass.ds(ti * D, D)]
            layer_norm(xin)
            quantise(hN, hN[:], D, P, xq, xq[:])
            wait("DVE", sx.free)
            wait("DVE", qs.full)
            done("DVE", V.tensor_copy(sx[:, 0:1], qs[:, 2:3]), sx.full, qs.free)
            ps = banks.take()
            wait("PE", ps.free)
            wait("PE", xq.full)
            wait("PE", identb.full)
            pb = ps[:].bitcast(BF16)
            for k in range(DC):
                ins = T.transpose(pb[:, k * P:(k + 1) * P], xq[:, k * P:(k + 1) * P], identb[:])
            done("PE", ins, ps.full, xq.free)
            wait("ACT", xqT.free)
            evac(xqT, xqT[:], ps, pb[:, 0:D], "ACT")
            wait("PE", xqT.full)
            wait("ACT DVE", sx.full)
            wait("ACT", gb.free)
            wait("DVE", ub.free)
            for o, n in FCOLS:
                ps = banks.take()
                wait("PE", ps.free)
                wait("PE", qwg.full)
                wait("PE", qwu.full)
                matmuls([(ps[:, 0:n], [(xqT[:, k * P:(k + 1) * P], qwg[:, k * FI + o:k * FI + o + n]) for k in range(DC)])], ps.full, xqT.free)
                wait("ACT", ps.full)
                done("ACT", A.activation(gb[:, o:o + n], ps[:, 0:n], ACT.Copy, scale=sx[:, 0:1]), gb.full, ps.free, sx.free)
                ps = banks.take()
                wait("PE", ps.free)
                matmuls([(ps[:, 0:n], [(xqT[:, k * P:(k + 1) * P], qwu[:, k * FI + o:k * FI + o + n]) for k in range(DC)])], ps.full, xqT.free)
                wait("DVE", ps.full)
                wait("DVE", wsu.full)
                done("DVE", V.scalar_tensor_tensor(ub[:, o:o + n], ps[:, 0:n], sx[:, 0:1], wsu[:, o:o + n], ALU.mult, ALU.mult), ub.full, ps.free, sx.free)
            wait("POOL", wsg.full)
            wait("POOL", gb.full)
            done("POOL", G.tensor_tensor(gb[:], gb[:], wsg[:], ALU.mult), gb.full)
            wait("ACT", gb.full)
            done("ACT", A.activation(gb[:], gb[:], ACT.Silu), gb.full)
            wait("DVE", gb.full)
            wait("DVE", ub.full)
            done("DVE", V.tensor_tensor(ub[:], ub[:], gb[:], ALU.mult), ub.full, gb.free)
            quantise(ub, ub[:], FI, P, tq, tq[:])
            wait("DVE", qs.full)
            done("DVE", V.tensor_copy(sx[:, 1:2], qs[:, 2:3]), sx.full, qs.free)
            wait("ACT", tqT.free)
            wait("PE", tq.full)
            for i in range(NT):
                ps = banks.take()
                wait("PE", ps.free)
                pb = ps[:].bitcast(BF16)
                for s, (o, n) in enumerate(FCH):
                    ins = T.transpose(pb[0:n, s * P:(s + 1) * P], tq[:, i * FT + o:i * FT + o + n], identb[:])
                done("PE", ins, ps.full, tq.free)
                evac(tqT, tqT[:, 3 * i * P:(3 * i + 2) * P], ps, pb[:, 0:2 * P], "ACT")
                evac(tqT, tqT[0:FCH[2][1], (3 * i + 2) * P:(3 * i + 3) * P], ps, pb[0:FCH[2][1], 2 * P:3 * P], "ACT")
            wait("PE", psO.free)
            wait("PE", tqT.full)
            wait("PE", qwd.full)
            matmuls([(psO[:], [(tqT[:, k * P:(k + 1) * P], qwd[:, k * D:(k + 1) * D]) for k in range(NFC)])], psO.full, tqT.free)
            wait("DVE", psO.full)
            wait("DVE", sx.full)
            wait("DVE", wsd.full)
            wait("DVE", ot.free)
            done("DVE", V.scalar_tensor_tensor(ot[:], psO[:], sx[:, 1:2], wsd[:], ALU.mult, ALU.mult), ot.full, psO.free, sx.free)
            wait("DVE", ot.full)
            done("DVE", V.tensor_tensor(ot[:], ot[:], xin, ALU.add), ot.full)
            wait("SP", ot.full)
            done("d_out", SP.dma_start(out.rearrange("b s d -> (b s) d")[bass.ds(ti * P, P), :], ot[:]), ot.free)
        c.wait_mark("SP", Mark(c.lines["d_out"], c.lines["d_out"].n, ()))
        return c.new


def constants():
    f = np.float32
    half = R // 2
    inv = (1.0 / 10000.0 ** (np.arange(half, dtype=np.float64) / half)).astype(f)
    ang = (np.arange(LK, dtype=f)[:, None] * inv).astype(f)
    cos, sin = np.cos(ang), np.sin(ang)
    ktab = np.concatenate([cos, cos, -sin, sin], axis=1).astype(f)
    q = np.arange(P)
    own = np.where((np.arange(GK)[None, :] % GQ) == (q[:, None] % GQ), 0.0, NEG)
    place = np.broadcast_to(np.arange(GK) // GQ, (P, GK))
    tiles = np.minimum(np.arange(NT + 1), NT) % NT
    return {
        "eye": np.eye(P, dtype=f),
        "tri": np.triu(np.ones((P, P), f)),
        "ktab": ktab,
        "qtab": np.concatenate([ktab[:S]] * B, axis=0),
        "pat": np.concatenate([own, place], axis=1).astype(f),
        "bstart": np.broadcast_to((tiles // TPB * LK).astype(f), (P, NT + 1)).copy(),
    }


NAMES = {
    "x": "x", "ctx": "ctx_2048", "itok": "itok_BxS_0_1023",
    "W_kvc": "L0_xattn_W_kvc", "W_dq": "L0_xattn_W_dq", "W_uq": "L0_xattn_W_uq", "W_qr": "L0_xattn_W_qr",
    "W_uk": "L0_xattn_W_uk", "W_kr": "L0_xattn_W_kr", "W_uv": "L0_xattn_W_uv", "W_o": "L0_xattn_W_o",
    "Wq": "L0_attn_Wq", "Wk": "L0_attn_Wk", "Wv": "L0_attn_Wv", "Wo": "L0_attn_Wo",
    "w_gate": "L0_ffn_w_gate", "w_up": "L0_ffn_w_up", "w_down": "L0_ffn_w_down",
    "d_idx": "L0_ffn_down_reorder_index",
}


def kernel(**inputs):
    import concourse.bacc as bacc
    from concourse.bass_utils import run_bass_kernel_spmd as run

    arrays = {"in_" + k: np.ascontiguousarray(inputs[v]) for k, v in NAMES.items()}
    arrays.update({"in_" + k: v for k, v in constants().items()})

    def program(plan):
        nc = bacc.Bacc("TRN2", target_bir_lowering=False, num_devices=1)
        a = {k[3:]: nc.dram_tensor(k, v.shape, mybir.dt.from_np(v.dtype), kind="ExternalInput").ap()
             for k, v in arrays.items()}
        out = nc.dram_tensor("out_0", (B, S, D), F32, kind="ExternalOutput").ap()
        return nc, build(nc, a, out, plan)

    _, plan = program({"K": {}, "opened": {}})
    nc, _ = program(plan)
    r = run(nc, [arrays], core_ids=[0])
    return r.results[0]["out_0"]
```

```python
from contextlib import ExitStack, contextmanager

import numpy as np
import concourse.bass as bass
from concourse import mybir

F32 = mybir.dt.float32
BF16 = mybir.dt.bfloat16
I32 = mybir.dt.int32
U32 = mybir.dt.uint32
ALU = mybir.AluOpType
ACT = mybir.ActivationFunctionType
AX = mybir.AxisListType

P = 128
B, S, D = 2, 256, 512
LK = 4096
NT = B * S // P
TPB = S // P
DC = D // P
H, HD, KVC, QC, R = 16, 128, 128, 192, 64
QLO, QHI = P, QC - P
LOOKBACK = 8
WIN = LOOKBACK + 1
GQ = P // H
NG = P // GQ
GK = WIN * GQ
GN = 96
XSCALE = 1.0 / float(np.sqrt(np.float32(HD + R)))
NEG = -1e30
NH, NKV, AD = 16, 8, 64
REP = NH // NKV
SOFTCAP = 50.0
ASCALE = 256.0 ** -0.5
VW = 96
FI = 1408
FT = FI // NT
FCH = [(0, 128), (128, 128), (256, 96)]
NFC = NT * len(FCH)
FP8_MAX = 448.0
EPS = 1e-5


class Line:

    def __init__(self, name, sem, step):
        self.name, self.sem, self.step, self.n, self.base = name, sem, step, 0, 0


class Mark:

    def __init__(self, line, n, path):
        self.line, self.n, self.path = line, n, path


class Counter:
    def __init__(self, nc, es, plan):
        self.nc, self.es, self.plan = nc, es, plan
        self.new = {"K": {}, "opened": {}}
        self.lines, self.gates, self.stack, self.iters = {}, [], [], {}
        self.seen = {}
        self.eng = {"PE": nc.tensor, "ACT": nc.scalar, "DVE": nc.vector, "POOL": nc.gpsimd, "SP": nc.sync}
        self.spare = es.enter_context(nc.semaphore("s_spare"))
        for e in ("PE", "ACT", "DVE", "POOL"):
            self.line(e, 1)

    def line(self, name, step, software=False):
        assert not self.stack, "a line has to be made outside of the loops"
        ln = Line(name, self.es.enter_context(self.nc.semaphore("s_" + name)), step)
        self.lines[name] = ln
        off = 0 if software else max([k.get(name, 0) for k in self.plan["K"].values()] + [0])
        if off:
            self.nc.sync.sem_inc(ln.sem, off)
        ln.base = off
        return ln

    @property
    def path(self):
        return tuple(x[0] for x in self.stack)

    def done(self, line, ins, *gates):
        ln = self.lines[line]
        ins.then_inc(ln.sem, ln.step)
        ln.n += ln.step
        m = Mark(ln, ln.n, self.path)
        for g in gates:
            g.opened[-1][line] = m
        return m

    def wait(self, engs, *gates):
        for e in engs.split():
            for g in gates:
                for d in range(len(g.opened) - 1, -1, -1):
                    for m in g.opened[d].values():
                        self.wait_mark(e, m)
                    if g.opened[d]:
                        break
                    if d > 0:
                        for m in self.plan["opened"].get(self.stack[d - 1][0], {}).get(g.name, {}).values():
                            self.wait_mark(e, m, prev=True)

    def wait_mark(self, eng, mark, prev=False):
        key = (eng, mark.line.name, mark.path, prev)
        if self.seen.get(key, -1) >= mark.n:
            return
        self.seen[key] = mark.n
        ln = self.lines[mark.line.name]
        v = mark.n + ln.base
        active = {x[0]: x[1] for x in self.stack}
        expr = None
        for lp in mark.path:
            k = self.plan["K"].get(lp, {}).get(mark.line.name, 0)
            if lp in active:
                if k:
                    expr = active[lp] * k if expr is None else expr + active[lp] * k
            else:
                v += (self.iters[lp] - 1) * k
        if prev:
            v -= self.plan["K"].get(mark.path[-1], {}).get(mark.line.name, 0)
        self.eng[eng].wait_ge(ln.sem, v if expr is None else expr + v)
        if eng == "SP":
            self.hold(eng)

    def hold(self, *engs):
        for e in engs:
            self.eng[e].sem_inc(self.spare, 1)

    @contextmanager
    def loop(self, name, n):
        if self.stack:
            self.hold(*self.eng)
        start = {k: ln.n for k, ln in self.lines.items()}
        with self.nc.Fori(0, n) as i:
            self.iters[name] = n
            self.stack.append((name, i))
            self.seen = {}
            for g in self.gates:
                g.opened.append({})
            yield i
            self.new["opened"][name] = {}
            for g in self.gates:
                inner = g.opened.pop()
                if inner:
                    self.new["opened"][name][g.name] = inner
                    g.opened[-1].update(inner)
            self.stack.pop()
            self.seen = {}
        ks = {}
        for k, ln in self.lines.items():
            d = ln.n - start.get(k, ln.n)
            ks[k] = d
            ln.n += d * (n - 1)
        self.new["K"][name] = ks


class Gate:

    def __init__(self, c, name):
        self.name = name
        self.opened = [{} for _ in range(len(c.stack) + 1)]
        c.gates.append(self)


class Buf:

    def __init__(self, c, name, t):
        self.c, self.name, self.t = c, name, t
        self.full, self.free = Gate(c, name + " full"), Gate(c, name + " free")

    def __getitem__(self, k):
        return self.t[k]


class Ring:

    def __init__(self, bufs):
        self.bufs, self.i, self.depth = bufs, 0, None

    def take(self):
        c = self.bufs[0].c
        if self.depth != c.path:
            self.depth, self.i = c.path, 0
        b = self.bufs[self.i % len(self.bufs)]
        self.i += 1
        return b


def build(nc, a, out, plan):
    with ExitStack() as es:
        c = Counter(nc, es, plan)
        T, A, V, G, SP = nc.tensor, nc.scalar, nc.vector, nc.gpsimd, nc.sync

        def sb(name, shape, dt=F32, scope=None):
            return Buf(c, name, (scope or es).enter_context(nc.sbuf_tensor(name, shape, dt)))

        banks = Ring([Buf(c, f"ps{i}", es.enter_context(nc.psum_tensor(f"ps{i}", [P, 512], F32))) for i in range(7)])
        psO = Buf(c, "psO", es.enter_context(nc.psum_tensor("psO", [P, 512], F32)))

        def dma_line(buf, software=False):
            ln = "d_" + buf.name
            if ln not in c.lines:
                c.line(ln, 16, software)
            return ln

        def load(buf, dst, src, eng="SP"):
            ln = dma_line(buf)
            h = c.eng[eng]
            with nc.allow_non_contiguous_dma(reason="strided weight or index layouts"):
                return c.done(ln, h.dma_start(dst, src), buf.full)

        wait, done = c.wait, c.done

        turn = [0]

        def evac(dst, dst_ap, bank, bank_ap, eng=None):
            if eng is None:
                eng = ("ACT", "DVE")[turn[0] % 2]
                turn[0] += 1
            wait(eng, bank.full)
            if eng == "ACT":
                ins = A.activation(dst_ap, bank_ap, ACT.Copy)
            else:
                ins = V.tensor_copy(dst_ap, bank_ap)
            return done(eng, ins, dst.full, bank.free)

        ident = sb("ident", [P, P])
        x1 = sb("x1", [P, NT * D])
        tab = sb("tab", [P, NT * P])
        half = sb("half", [P, 1])
        hN = sb("hN", [P, D])
        hT = sb("hT", [P, D])
        st = sb("st", [P, 12])
        wq = sb("wq", [P, DC * NH * AD])

        load(ident, ident[:], a["eye"])
        load(x1, x1[:].rearrange("p (t d) -> p t d", t=NT), a["x"].rearrange("b (t p) d -> p (b t) d", p=P))
        done("POOL", G.memset(half[:], -0.5), half.full)

        def layer_norm(xin, st=st, hN=hN):
            wait("DVE", x1.full)
            wait("POOL", half.full)
            wait("DVE", st.free)
            done("DVE", V.bn_stats(st[:, 0:6], xin), st.full)
            wait("DVE", st.full)
            c.hold("DVE")
            done("DVE", V.bn_aggr(st[:, 6:8], st[:, 0:6]), st.full)
            wait("DVE", st.full)
            done("DVE", V.tensor_scalar(st[:, 8:9], st[:, 7:8], EPS, None, ALU.add), st.full)
            wait("POOL", st.full)
            done("POOL", G.tensor_tensor(st[:, 9:10], st[:, 8:9], half[:], ALU.pow), st.full)
            wait("DVE", hN.free)
            wait("DVE", st.full)
            done("DVE", V.tensor_scalar(hN[:], xin, st[:, 6:7], st[:, 9:10], ALU.subtract, ALU.mult), hN.full, st.free, x1.free)

        def transpose_h():
            ps = banks.take()
            wait("PE", ps.free)
            wait("PE", hN.full)
            wait("PE", ident.full)
            for k in range(DC):
                ins = T.transpose(ps[:, k * P:(k + 1) * P], hN[:, k * P:(k + 1) * P], ident[:])
            done("PE", ins, ps.full, hN.free)
            wait("ACT", hT.free)
            evac(hT, hT[:], ps, ps[:], "ACT")

        def matmuls(parts, *gates):
            for o, terms in parts:
                for n, (l, rh) in enumerate(terms):
                    ins = T.matmul(o, l, rh, start=n == 0, stop=n == len(terms) - 1)
            return done("PE", ins, *gates)

        def rope(ps, heads, cs, sn, ra, rb, dst, dst_ap):
            hf = AD // 2
            xv = ps[:, 0:heads * AD].rearrange("p (h d) -> p h d", h=heads)
            av = ra[:, 0:heads * AD].rearrange("p (h d) -> p h d", h=heads)
            bv = rb[:, 0:heads * AD].rearrange("p (h d) -> p h d", h=heads)
            wait("DVE", ps.full)
            wait("DVE", tab.full)
            wait("DVE", ra.free)
            wait("DVE", rb.free)
            done("DVE", V.tensor_tensor(av, xv, cs.unsqueeze(1).to_broadcast([P, heads, AD]), ALU.mult), ra.full)
            for d0, s0 in ((0, hf), (hf, 0)):
                m = done("DVE", V.tensor_tensor(bv[:, :, d0:d0 + hf], xv[:, :, s0:s0 + hf],
                                              sn[:, d0:d0 + hf].unsqueeze(1).to_broadcast([P, heads, hf]), ALU.mult), rb.full, ps.free)
            wait("POOL", ra.full)
            wait("POOL", rb.full)
            done("POOL", G.tensor_tensor(dst_ap.rearrange("p (h c d) -> p h c d", h=heads, c=2),
                                       av.unsqueeze(2).to_broadcast([P, heads, 2, AD]),
                                       bv.unsqueeze(2).to_broadcast([P, heads, 2, AD]), ALU.add), dst.full, ra.free, rb.free)

        with ExitStack() as xs:
            xsb = lambda n, s, d=F32: sb(n, s, d, xs)
            g_lo = xsb("g_lo", [P, H * KVC])
            g_hi = xsb("g_hi", [P, H * KVC])
            vo = xsb("vo", [P, H * D])
            wqr_lo = xsb("wqr_lo", [P, H * R])
            wqr_hi = xsb("wqr_hi", [P, H * R])
            wdq = xsb("wdq", [P, DC * QC])
            wkvc = xsb("wkvc", [P, DC * KVC])
            wkr = xsb("wkr", [P, 2 * R])
            cg = xsb("cg", [P, WIN * D])
            rt = xsb("rt", [P, WIN * 2 * R])
            segi = xsb("segi", [P, NT], I32)
            seg = xsb("seg", [P, NT + 1])
            beg = xsb("beg", [P, NT + 1])
            upos = xsb("upos", [P, NT])
            idxc = xsb("idxc", [P, 1], I32)
            idxr = xsb("idxr", [P, 1], I32)
            bstart = xsb("bstart", [P, NT + 1])
            pat = xsb("pat", [P, 2 * GK])
            msk = xsb("msk", [P, GN], BF16)
            mtmp = xsb("mtmp", [P, 2 * GK])
            eg = xsb("eg", [P, NG * P], BF16)

            load(segi, segi[:], a["itok"].rearrange("b (t p) -> p (b t)", p=P))
            load(bstart, bstart[:], a["bstart"])
            load(pat, pat[:], a["pat"])
            load(wdq, wdq[:].rearrange("p (k n) -> p k n", k=DC), a["W_dq"].rearrange("(k p) n -> p k n", p=P))

            wait("DVE", segi.full)
            wait("DVE", bstart.full)
            done("DVE", V.tensor_copy(seg[:, 0:NT], segi[:]), seg.full)
            wait("DVE", seg.full)
            done("DVE", V.tensor_copy(seg[:, NT:NT + 1], seg[:, 0:1]), seg.full)
            wait("DVE", seg.full)
            done("DVE", V.tensor_scalar(beg[:], seg[:], -float(LOOKBACK), 0.0, ALU.add, ALU.max), beg.full)
            wait("DVE", beg.full)
            done("DVE", V.tensor_scalar(beg[:], beg[:], float(LK - WIN), None, ALU.min), beg.full)
            wait("DVE", beg.full)
            done("DVE", V.tensor_tensor(upos[:], seg[:, 0:NT], beg[:, 0:NT], ALU.subtract), upos.full)

            def gather(t):
                wait("DVE", beg.full)
                wait("DVE", idxc.free)
                wait("DVE", idxr.free)
                done("DVE", V.tensor_tensor(idxc[:], beg[:, bass.ds(t, 1)], bstart[:, bass.ds(t, 1)], ALU.add), idxc.full)
                done("DVE", V.tensor_copy(idxr[:], beg[:, bass.ds(t, 1)]), idxr.full)
                for buf, idx, src in ((cg, idxc, a["ctx"].rearrange("b s d -> (b s) d")), (rt, idxr, a["ktab"])):
                    ln = dma_line(buf, software=True)
                    wait("POOL", buf.free)
                    wait("POOL", idx.full)
                    c.hold("POOL")
                    done(ln, G.indirect_dma_start(buf[:], None, src, bass.IndirectOffsetOnAxis(ap=idx[:, 0:1], axis=0)),
                         buf.full, idx.free)

            gather(0)

            load(tab, tab[:].rearrange("p (t d) -> p t d", t=NT), a["qtab"].rearrange("(t p) d -> p t d", p=P))
            load(wkvc, wkvc[:].rearrange("p (k n) -> p k n", k=DC), a["W_kvc"].rearrange("(k p) n -> p k n", p=P))
            load(wkr, wkr[:, 0:R], a["W_kr"])
            load(wkr, wkr[:, R:R + R // 2], a["W_kr"][:, R // 2:R])
            load(wkr, wkr[:, R + R // 2:2 * R], a["W_kr"][:, 0:R // 2])
            load(wqr_lo, wqr_lo[:], a["W_qr"][0:QLO, :])
            done("POOL", G.memset(wqr_hi[:], 0.0), wqr_hi.full)
            wait("SP", wqr_hi.full)
            load(wqr_hi, wqr_hi[0:QHI, :], a["W_qr"][QLO:QC, :])
            done("POOL", G.memset(g_hi[:], 0.0), g_hi.full)
            done("POOL", G.memset(msk[:], 0.0), msk.full)
            wait("DVE", ident.full)
            done("DVE", V.tensor_copy(eg[:].rearrange("p (q h) -> p q h", h=H),
                                    ident[:].unsqueeze(2).to_broadcast([P, P, H])), eg.full)

            with ExitStack() as hs:
                HU = 4
                sets = [dict(uq_lo=sb(f"uq_lo{s}", [P, HD], F32, hs), uq_hi=sb(f"uq_hi{s}", [QHI, HD], F32, hs),
                             uk=sb(f"uk{s}", [KVC, HD], F32, hs), uv=sb(f"uv{s}", [KVC, HD], F32, hs),
                             wo=sb(f"wo{s}", [HD, D], F32, hs)) for s in range(HU)]
                tw = Ring([sb(f"tw{i}", [P, 2 * P + QC], F32, hs) for i in range(2)])
                wait("DVE", g_hi.full)
                for w in sets:
                    for buf in w.values():
                        dma_line(buf)
                with c.loop("heads", H // HU) as hi:
                    for s in range(HU):
                        w = sets[s]
                        col = hi * (HU * HD) + s * HD
                        for k, src in (("uq_lo", a["W_uq"][0:QLO, bass.ds(col, HD)]),
                                       ("uq_hi", a["W_uq"][QLO:QC, bass.ds(col, HD)]),
                                       ("uk", a["W_uk"][:, bass.ds(col, HD)]),
                                       ("uv", a["W_uv"][:, bass.ds(col, HD)]),
                                       ("wo", a["W_o"][bass.ds(col, HD), :])):
                            wait("SP", w[k].free)
                            load(w[k], w[k][:], src)
                        ps = banks.take()
                        wait("PE", ps.free)
                        for k, o, n in (("uq_lo", 0, P), ("uq_hi", P, QHI), ("uk", QC, P), ("uv", QC + P, P)):
                            wait("PE", w[k].full)
                            c.hold("PE")
                            m = done("PE", T.transpose(ps[:, o:o + n], w[k][:], ident[0:n, 0:n]), ps.full, w[k].free)
                        t = tw.take()
                        wait("ACT", t.free)
                        evac(t, t[:], ps, ps[:, 0:2 * P + QC], "ACT")
                        wait("PE", t.full)
                        pg = banks.take()
                        wait("PE", pg.free)
                        matmuls([(pg[:, 0:P], [(t[:, 0:P], t[:, QC:QC + P])]),
                                     (pg[0:QHI, P:2 * P], [(t[:, P:QC], t[:, QC:QC + P])])], pg.full, t.free)
                        evac(g_lo, g_lo[:, bass.ds(col, P)], pg, pg[:, 0:P], "DVE")
                        evac(g_hi, g_hi[0:QHI, bass.ds(col, P)], pg, pg[0:QHI, P:2 * P], "DVE")
                        pv = banks.take()
                        wait("PE", pv.free)
                        wait("PE", w["wo"].full)
                        matmuls([(pv[:], [(t[:, QC + P:QC + 2 * P], w["wo"][:])])], pv.full, t.free, w["wo"].free)
                        evac(vo, vo[:, bass.ds(hi * (HU * D) + s * D, D)], pv, pv[:], ("ACT", "DVE")[s % 2])

            for e in ("PE", "ACT", "DVE", "POOL", "SP"):
                for o in ("PE", "ACT", "DVE"):
                    c.wait_mark(e, Mark(c.lines[o], c.lines[o].n, ()))
            load(wq, wq[:].rearrange("p (k n) -> p k n", k=DC), a["Wq"].rearrange("(k p) n -> p k n", p=P))

            qc = xsb("qc", [P, 2 * P])
            ct = Ring([xsb(f"ct{i}", [P, DC * 3 * P]) for i in range(2)])
            kc = xsb("kc", [P, NG * GK + GN - GK])
            kr = xsb("kr", [P, NG * GK + GN - GK])
            rtT = xsb("rtT", [P, WIN * P])
            kn = xsb("kn", [P, NG * KVC])
            pt = Ring([xsb(f"pt{i}", [P, 4 * P]) for i in range(2)])
            pr = Ring([xsb(f"pr{i}", [P, 4 * GK]) for i in range(2)])
            sm = Ring([xsb(f"sm{i}", [P, 12]) for i in range(2)])
            qa = xsb("qa", [P, P * H])
            qr = xsb("qr", [P, P * H])
            qn = xsb("qn", [P, H * 2 * R])
            oc = xsb("oc", [P, P * H])
            ra, rb = xsb("ra", [P, 512]), xsb("rb", [P, 512])
            done("POOL", G.memset(qc[:], 0.0), qc.full)
            done("POOL", G.memset(kn[:], 0.0), kn.full)
            for b_ in pt.bufs:
                done("POOL", G.memset(b_[:], 0.0), b_.full)
            for b_ in (kc, kr):
                zeroed = done("POOL", G.memset(b_[:, NG * GK:], 0.0), b_.full)
            for e in ("PE", "ACT", "DVE"):
                c.wait_mark(e, zeroed)

            def by_hq(buf, h0, n):
                return buf[:].rearrange("p (q h) -> p h q", h=H)[:, h0:h0 + n, :]

            with c.loop("tiles", NT) as ti:
                xin = x1[:, bass.ds(ti * D, D)]
                layer_norm(xin)
                transpose_h()

                wait("DVE", mtmp.free)
                wait("DVE", msk.free)
                uc = upos[:, bass.ds(ti, 1)]
                done("DVE", V.tensor_scalar(mtmp[:, 0:GK], pat[:, GK:], uc, NEG, ALU.is_gt, ALU.mult), mtmp.full)
                done("DVE", V.tensor_scalar(mtmp[:, GK:], pat[:, GK:], uc, -float(LOOKBACK), ALU.subtract, ALU.is_lt), mtmp.full)
                wait("DVE", mtmp.full)
                m1 = done("DVE", V.scalar_tensor_tensor(mtmp[:, GK:], mtmp[:, GK:], NEG, mtmp[:, 0:GK], ALU.mult, ALU.add), mtmp.full)
                wait("DVE", mtmp.full)
                done("DVE", V.tensor_tensor(msk[:, 0:GK], mtmp[:, GK:], pat[:, 0:GK], ALU.add), msk.full, mtmp.free)

                wait("PE", cg.full)
                wait("ACT DVE", kc.free)
                for s in range(WIN // 3):
                    cb = ct.take()
                    wait("ACT DVE", cb.free)
                    for jj in range(3):
                        ps = banks.take()
                        wait("PE", ps.free)
                        for k in range(DC):
                            o = (3 * s + jj) * D + k * P
                            ins = T.transpose(ps[:, k * P:(k + 1) * P], cg[:, o:o + P], ident[:])
                        done("PE", ins, ps.full, cg.free)
                        evac(cb, cb[:].rearrange("p (k j q) -> p k j q", k=DC, j=3)[:, :, jj, :], ps,
                             ps[:].rearrange("p (k q) -> p k q", k=DC))
                    ps = banks.take()
                    wait("PE", ps.free)
                    wait("PE", cb.full)
                    wait("PE", wkvc.full)
                    matmuls([(ps[:, 0:3 * P], [(wkvc[:, k * KVC:(k + 1) * KVC], cb[:, k * 3 * P:(k + 1) * 3 * P])
                                                   for k in range(DC)])], ps.full, cb.free)
                    src = ps[:, 0:3 * P].rearrange("p (j g q) -> p j g q", j=3, g=NG)
                    dst = kc[:, 0:NG * GK].rearrange("p (g j q) -> p j g q", g=NG, j=WIN)[:, 3 * s:3 * s + 3]
                    evac(kc, dst, ps, src, "DVE")

                wait("PE", rt.full)
                wait("ACT DVE", rtT.free)
                for s in range(WIN // 3):
                    ps = banks.take()
                    wait("PE", ps.free)
                    for jj in range(3):
                        ins = T.transpose(ps[:, jj * P:(jj + 1) * P], rt[:, (3 * s + jj) * P:(3 * s + jj + 1) * P], ident[:])
                    done("PE", ins, ps.full, rt.free)
                    evac(rtT, rtT[:].rearrange("p (g j q) -> p j g q", g=NG, j=WIN)[:, 3 * s:3 * s + 3], ps,
                         ps[:, 0:3 * P].rearrange("p (j g q) -> p j g q", j=3, g=NG))

                gather(ti + 1)

                pq = banks.take()
                wait("PE", pq.free)
                wait("PE", hT.full)
                wait("PE", wdq.full)
                matmuls([(pq[:, 0:P], [(wdq[:, k * QC:k * QC + QLO], hT[:, k * P:(k + 1) * P]) for k in range(DC)]),
                             (pq[0:QHI, P:2 * P], [(wdq[:, k * QC + QLO:(k + 1) * QC], hT[:, k * P:(k + 1) * P])
                                                   for k in range(DC)])], pq.full, hT.free)
                wait("ACT", qc.free)
                evac(qc, qc[:, 0:P], pq, pq[:, 0:P], "ACT")
                evac(qc, qc[0:QHI, P:2 * P], pq, pq[0:QHI, P:2 * P], "ACT")

                wait("PE", qc.full)
                wait("PE", wqr_lo.full)
                wait("PE", wqr_hi.full)
                wait("POOL", qn.free)
                tb = tab[:, bass.ds(ti * P, P)]
                for n in range(2):
                    ps = banks.take()
                    wait("PE", ps.free)
                    matmuls([(ps[:], [(qc[:, 0:P], wqr_lo[:, n * 512:(n + 1) * 512]),
                                          (qc[:, P:2 * P], wqr_hi[:, n * 512:(n + 1) * 512])])], ps.full, qc.free)
                    rope(ps, 8, tab[:, bass.ds(ti * P, AD)], tab[:, bass.ds(ti * P + AD, AD)], ra, rb,
                         qn, qn[:, n * 1024:(n + 1) * 1024])

                wait("ACT DVE", qa.free)
                for n in range(4):
                    ps = banks.take()
                    wait("PE", ps.free)
                    matmuls([(ps[:, i * P:(i + 1) * P],
                                  [(g_lo[:, h * P:(h + 1) * P], qc[:, 0:P]), (g_hi[:, h * P:(h + 1) * P], qc[:, P:2 * P])])
                                 for i, h in enumerate(range(4 * n, 4 * n + 4))], ps.full, qc.free)
                    evac(qa, by_hq(qa, 4 * n, 4), ps, ps[:].rearrange("p (h q) -> p h q", h=4))

                wait("DVE", rtT.full)
                wait("PE", kc.full)
                wait("PE", wkr.full)
                wait("DVE", kr.free)
                for s in range(WIN // 3):
                    ps = banks.take()
                    wait("PE", ps.free)
                    matmuls([(ps[:, 0:3 * P], [(wkr[:], kc[:, s * 3 * P:(s + 1) * 3 * P])])], ps.full, kc.free)
                    wait("DVE", ps.full)
                    done("DVE", V.tensor_tensor(kr[:, s * 3 * P:(s + 1) * 3 * P], ps[:, 0:3 * P],
                                              rtT[:, s * 3 * P:(s + 1) * 3 * P], ALU.mult), kr.full, ps.free, rtT.free)

                wait("ACT DVE", qr.free)
                wait("PE", qn.full)
                for n in range(4):
                    ps = banks.take()
                    wait("PE", ps.free)
                    for i in range(4):
                        ins = T.transpose(ps[:, i * P:(i + 1) * P], qn[:, (4 * n + i) * P:(4 * n + i + 1) * P], ident[:])
                    done("PE", ins, ps.full, qn.free)
                    evac(qr, by_hq(qr, 4 * n, 4), ps, ps[:].rearrange("p (h q) -> p h q", h=4))

                wait("PE", qa.full)
                wait("PE", qr.full)
                wait("PE", kr.full)
                wait("PE", msk.full)
                wait("PE", eg.full)

                def scores(n):
                    ps = banks.take()
                    wait("PE", ps.free)
                    matmuls([(ps[:, i * GN:(i + 1) * GN],
                                  [(eg[:, g * P:(g + 1) * P], msk[:]),
                                   (qa[:, g * P:(g + 1) * P], kc[:, g * GK:g * GK + GN]),
                                   (qr[:, g * P:(g + 1) * P], kr[:, g * GK:g * GK + GN])])
                                 for i, g in enumerate(range(4 * n, 4 * n + 4))], ps.full, qa.free, qr.free, kc.free, kr.free, msk.free)
                    p, s = pr.take(), sm.take()
                    sv = ps[:, 0:4 * GN].rearrange("p (g k) -> p g k", g=4)[:, :, 0:GK]
                    pv = p[:].rearrange("p (g k) -> p g k", g=4)
                    wait("DVE", ps.full)
                    wait("DVE", s.free)
                    wait("DVE", p.free)
                    done("DVE", V.tensor_reduce(s[:, 0:4], sv, AX.X, ALU.max), s.full)
                    wait("DVE", s.full)
                    done("DVE", V.tensor_tensor(pv, sv, s[:, 0:4].unsqueeze(2).to_broadcast([P, 4, GK]), ALU.subtract), p.full, ps.free)
                    wait("ACT", p.full)
                    done("ACT", A.activation(p[:], p[:], ACT.Exp, scale=XSCALE), p.full)
                    wait("DVE", p.full)
                    done("DVE", V.tensor_reduce(s[:, 4:8], pv, AX.X, ALU.add), s.full)
                    wait("DVE", s.full)
                    done("DVE", V.reciprocal(s[:, 8:12], s[:, 4:8]), s.full)
                    wait("POOL", s.full)
                    wait("POOL", p.full)
                    done("POOL", G.tensor_tensor(pv, pv, s[:, 8:12].unsqueeze(2).to_broadcast([P, 4, GK]), ALU.mult), p.full, s.free)
                    return p

                def values(n, p):
                    ps = banks.take()
                    wait("PE", ps.free)
                    wait("PE", p.full)
                    for i in range(4):
                        ins = T.transpose(ps[0:GK, i * P:(i + 1) * P], p[:, i * GK:(i + 1) * GK], ident[:])
                    done("PE", ins, ps.full, p.free)
                    q = pt.take()
                    wait("ACT", q.free)
                    evac(q, q[0:GK, :], ps, ps[0:GK, :], "ACT")
                    ps = banks.take()
                    wait("PE", ps.free)
                    wait("PE", q.full)
                    matmuls([(ps[:, i * P:(i + 1) * P], [(kn[:, (4 * n + i) * P:(4 * n + i + 1) * P],
                                                              q[:, i * P:(i + 1) * P])]) for i in range(4)], ps.full, q.free, kn.free)
                    evac(oc, oc[:, n * 512:(n + 1) * 512], ps, ps[:])

                def key_rows(n):
                    ps = banks.take()
                    wait("PE", ps.free)
                    for i in range(4):
                        g = 4 * n + i
                        ins = T.transpose(ps[0:GK, i * P:(i + 1) * P], kc[:, g * GK:(g + 1) * GK], ident[:])
                    done("PE", ins, ps.full, kc.free)
                    evac(kn, kn[0:GK, n * 512:(n + 1) * 512], ps, ps[0:GK, :])

                wait("ACT DVE", oc.free)
                wait("ACT DVE", kn.free)
                p0 = scores(0)
                key_rows(0)
                p1 = scores(1)
                key_rows(1)
                key_rows(2)
                wait("PE", kn.full)
                values(0, p0)
                p2 = scores(2)
                key_rows(3)
                wait("PE", kn.full)
                values(1, p1)
                p3 = scores(3)
                values(2, p2)
                values(3, p3)

                wait("PE", psO.free)
                wait("PE", oc.full)
                wait("PE", vo.full)
                ov = oc[:].rearrange("p (q h) -> p h q", h=H)
                matmuls([(psO[:], [(ov[:, h, :], vo[:, h * D:(h + 1) * D]) for h in range(H)])], psO.full, oc.free)
                wait("DVE", psO.full)
                done("DVE", V.tensor_tensor(xin, psO[:], xin, ALU.add), x1.full, psO.free)

        for e in ("PE", "ACT", "DVE", "POOL", "SP"):
            for o in ("PE", "ACT", "DVE", "POOL", "d_cg", "d_rt"):
                c.wait_mark(e, Mark(c.lines[o], c.lines[o].n, ()))

        qwg = sb("qwg", [P, DC * FI], BF16)
        qwu = sb("qwu", [P, DC * FI], BF16)
        qwd = sb("qwd", [P, NFC * D], BF16)
        wsg = sb("wsg", [P, FI])
        wsu = sb("wsu", [P, FI])
        wsd = sb("wsd", [P, D])
        identb = sb("identb", [P, P], BF16)
        ones = sb("ones", [P, P])
        done("DVE", V.tensor_copy(identb[:], ident[:]), identb.full)
        done("POOL", G.memset(ones[:], 1.0), ones.full)
        zeroed = done("POOL", G.memset(qwd[:], 0.0), qwd.full)

        def quant_top(src, src_ap, segs, s):
            rows = src_ap.shape[0]
            sv = src_ap.rearrange("p (s n) -> p s n", s=segs)
            top, mul, inv, sc = (s[0:rows, i * 2:i * 2 + segs] for i in range(4))
            wait("DVE", src.full, s.free)
            done("DVE", V.tensor_reduce(top, sv, AX.X, ALU.max, apply_absolute_value=True), s.full)
            wait("DVE", s.full)
            done("DVE", V.reciprocal(inv, top), s.full)
            wait("DVE", s.full)
            done("DVE", V.tensor_scalar(mul, inv, FP8_MAX, None, ALU.mult), s.full)
            done("DVE", V.tensor_scalar(sc, top, 1.0 / FP8_MAX, None, ALU.mult), s.full)

        def quant_scale(src, src_ap, segs, y, y_ap, s, *gates):
            rows = src_ap.shape[0]
            sv = src_ap.rearrange("p (s n) -> p s n", s=segs)
            yv = y_ap.rearrange("p (s n) -> p s n", s=segs)
            mul = s[0:rows, 2:2 + segs]
            wait("ACT", src.full, s.full, y.free)
            for i in range(segs):
                done("ACT", A.activation(yv[:, i], sv[:, i], ACT.Copy, scale=mul[:, i:i + 1]), y.full, src.free, s.free, *gates)

        def quant_magic(y, y_ap, m, m_ap):
            wait("DVE", y.full, m.free)
            done("DVE", V.tensor_scalar(m_ap.bitcast(U32), y_ap.bitcast(U32), 0x7F800000, 0x00400000,
                                        ALU.bitwise_and, ALU.bitwise_or), m.full)
            wait("DVE", m.full)
            done("DVE", V.tensor_scalar(m_ap, m_ap, 1.5 * 2.0 ** -6, 2.0 ** 20, ALU.max, ALU.mult), m.full)
            wait("POOL", m.full, y.full)
            done("POOL", G.tensor_tensor(y_ap, y_ap, m_ap, ALU.add), y.full)

        def quant_out(y, y_ap, m, m_ap, dst, dst_ap):
            wait("DVE", y.full, m.full, dst.free)
            done("DVE", V.tensor_tensor(dst_ap, y_ap, m_ap, ALU.subtract), dst.full, y.free, m.free)

        def diagonal(s, scale_ap, rows, dg):
            wait("DVE", dg.free, s.full, ident.full)
            done("DVE", V.tensor_scalar(dg[0:rows, 0:rows], ident[0:rows, 0:rows], scale_ap, None, ALU.mult), dg.full, s.free)

        def spread(dg, rows, dst, dst_ap):
            ps = banks.take()
            wait("PE", ps.free, dg.full, ones.full)
            matmuls([(ps[:, 0:rows], [(ones[0:rows, :], dg[0:rows, 0:rows])])], ps.full, dg.free)
            evac(dst, dst_ap, ps, ps[:, 0:rows], "ACT")

        with ExitStack() as ss:
            ssb = lambda n, s, d=F32: sb(n, s, d, ss)
            wk, wv = ssb("wk", [P, DC * NKV * AD]), ssb("wv", [P, DC * NKV * AD])
            wao = ssb("wao", [P, 8 * D])
            sn = ssb("sn", [P, NH * 2 * AD])
            kn2 = ssb("kn2", [P, NKV * P])
            sa, sbb = ssb("sa", [P, 512]), ssb("sbb", [P, 512])
            qT = ssb("qT", [P, NH * S])
            kT = ssb("kT", [P, NKV * S])
            v1 = ssb("v1", [P, TPB * NKV * VW])
            px = Ring([ssb(f"px{i}", [P, 3 * REP * P]) for i in range(2)])
            tri = ssb("tri", [P, P])
            rden = Ring([ssb(f"rden{i}", [P, 2 * REP]) for i in range(2)])
            yn = ssb("yn", [P, TPB * NH * AD])
            yT = ssb("yT", [P, NH * AD])
            wr = [ssb(f"wr{i}", [P, FI]) for i in range(4)]
            wm = ssb("wm", [P, FI])
            wsc = [ssb(f"wsc{i}", [P, 8]) for i in range(3)]
            di = [ssb(f"di{i}", [P, 1], I32) for i in range(4)]
            wb = ssb("wb", [P, FI], BF16)
            dgs = [ssb(f"dg{i}", [P, P]) for i in range(2)]
            for buf in di:
                dma_line(buf)
            for buf in wr:
                if buf is wr[len(FCH)]:
                    c.line("d_" + buf.name, 16)
                else:
                    c.line("g_" + buf.name, 16, software=True)
            load(wk, wk[:].rearrange("p (k n) -> p k n", k=DC), a["Wk"].rearrange("(k p) n -> p k n", p=P))
            load(wv, wv[:].rearrange("p (k n) -> p k n", k=DC), a["Wv"].rearrange("(k p) n -> p k n", p=P))
            load(wao, wao[:].rearrange("p (k n) -> p k n", k=8), a["Wo"].rearrange("(k p) n -> p k n", p=P))
            load(tri, tri[:], a["tri"])
            v1v = v1[:].rearrange("p (x w) -> p x w", w=VW)
            done("DVE", V.memset(v1v[:, :, AD:AD + 1], 1.0), v1.full)
            vz = done("DVE", V.memset(v1v[:, :, AD + 1:], 0.0), v1.full)
            for e in ("PE", "ACT", "DVE"):
                c.wait_mark(e, vz)
                c.wait_mark(e, zeroed)

            NPC = TPB * (len(FCH) + 1)

            def piece(b, p):
                ti, s = b * TPB + p // (len(FCH) + 1), p % (len(FCH) + 1)
                o, n = FCH[s] if s < len(FCH) else (None, P)
                return ti, o, n, wr[p % 4], wm, wsc[p % 3]

            def fetch_index(b, p):
                ti, o, n, _, _, _ = piece(b, p)
                if o is not None:
                    d = di[p % 4]
                    wait("SP", d.free)
                    load(d, d[0:n, :], a["d_idx"].rearrange("(n o) -> n o", o=1)[bass.ds(ti * FT + o, n), :])

            def fetch(b, p):
                ti, o, n, w, _, _ = piece(b, p)
                if o is None:
                    wait("SP", w.free)
                    done("d_" + w.name, SP.dma_start(w[:], a["w_down"][bass.ds(ti * P, P), :]), w.full)
                    return
                d = di[p % 4]
                wait("POOL", w.free, d.full)
                for i, src in enumerate((a["w_gate"], a["w_up"])):
                    c.hold("POOL")
                    done("g_" + w.name, G.indirect_dma_start(w[0:n, i * D:(i + 1) * D], None, src,
                                                             bass.IndirectOffsetOnAxis(ap=d[0:n, 0:1], axis=0)), w.full)

            def piece_top(b, p):
                _, o, n, w, _, s = piece(b, p)
                quant_top(w, w[:] if o is None else w[0:n, 0:2 * D], 1 if o is None else 2, s)

            def piece_scale(b, p):
                _, o, n, w, _, s = piece(b, p)
                ap = w[:] if o is None else w[0:n, 0:2 * D]
                quant_scale(w, ap, 1 if o is None else 2, w, ap, s, *([] if o is None else [di[p % 4].free]))

            def piece_magic(b, p):
                _, o, n, w, m, _ = piece(b, p)
                e = FI if o is None else 2 * D
                quant_magic(w, w[0:n, 0:e], m, m[0:n, 0:e])

            def piece_out(b, p):
                _, o, n, w, m, s = piece(b, p)
                e = FI if o is None else 2 * D
                quant_out(w, w[0:n, 0:e], m, m[0:n, 0:e], wb, wb[0:n, 0:e])
                for i in range(1 if o is None else 2):
                    diagonal(s, s[0:n, 6 + i:7 + i], n, dgs[i])

            def piece_transpose(b, p):
                ti, o, n, _, _, s = piece(b, p)
                if o is None:
                    spread(dgs[0], P, wsd, wsd[:, bass.ds(ti * P, P)])
                    wait("PE", wb.full, identb.full)
                    for i in range(NT):
                        ps = banks.take()
                        wait("PE", ps.free)
                        pb = ps[:].bitcast(BF16)
                        for k, (o, n) in enumerate(FCH):
                            ins = T.transpose(pb[0:n, k * P:(k + 1) * P], wb[:, i * FT + o:i * FT + o + n], identb[:])
                        done("PE", ins, ps.full, wb.free)
                        qv = qwd[:].rearrange("p (c o) -> p c o", o=D)
                        pv = pb[:, 0:3 * P].rearrange("p (s o) -> p s o", s=3)
                        evac(qwd, qv[:, 3 * i:3 * i + 2, bass.ds(ti * P, P)], ps, pv[:, 0:2, :], "ACT")
                        evac(qwd, qv[0:FCH[2][1], 3 * i + 2, bass.ds(ti * P, P)], ps, pv[0:FCH[2][1], 2, :], "ACT")
                    return
                for i, (qw, ws) in enumerate(((qwg, wsg), (qwu, wsu))):
                    spread(dgs[i], n, ws, ws[:, bass.ds(ti * FT + o, n)])
                    ps = banks.take()
                    wait("PE", ps.free, wb.full, identb.full)
                    pb = ps[:].bitcast(BF16)
                    for k in range(DC):
                        ins = T.transpose(pb[:, k * P:k * P + n], wb[0:n, i * D + k * P:i * D + (k + 1) * P], identb[0:n, 0:n])
                    done("PE", ins, ps.full, wb.free)
                    evac(qw, qw[:].rearrange("p (k m) -> p k m", k=DC)[:, :, bass.ds(ti * FT + o, n)], ps,
                         pb[:, 0:DC * P].rearrange("p (k m) -> p k m", k=DC)[:, :, 0:n], "ACT")

            with c.loop("batches", B) as b:
                def slot(k, before=lambda: None):
                    if 0 <= k - 3 < NPC:
                        piece_transpose(b, k - 3)
                    before()
                    if 0 <= k - 1 < NPC:
                        piece_scale(b, k - 1)
                    if 0 <= k - 2 < NPC:
                        piece_out(b, k - 2)
                    if k + 2 < NPC:
                        fetch(b, k + 2)
                    if 0 <= k - 1 < NPC:
                        piece_magic(b, k - 1)
                    if k < NPC:
                        piece_top(b, k)
                    if k + 3 < NPC:
                        fetch_index(b, k + 3)

                def project(t, between):
                    ti = b * TPB + t
                    cos, sin = tab[:, bass.ds(ti * P, AD)], tab[:, bass.ds(ti * P + AD, AD)]
                    wait("PE", hT.full, wq.full, wk.full, wv.full)
                    wait("POOL", sn.free)
                    for n in range(2):
                        ps = banks.take()
                        wait("PE", ps.free)
                        matmuls([(ps[:], [(hT[:, k * P:(k + 1) * P], wq[:, k * 1024 + n * 512:k * 1024 + (n + 1) * 512])
                                          for k in range(DC)])], ps.full, hT.free)
                        rope(ps, 8, cos, sin, sa, sbb, sn, sn[:, n * 1024:(n + 1) * 1024])
                    ps = banks.take()
                    wait("PE", ps.free)
                    matmuls([(ps[:], [(hT[:, k * P:(k + 1) * P], wk[:, k * 512:(k + 1) * 512]) for k in range(DC)])], ps.full, hT.free)
                    wait("DVE", ps.full, kn2.free)
                    kv = ps[:].rearrange("p (h d) -> p h d", h=NKV)
                    ko = kn2[:].rearrange("p (h d) -> p h d", h=NKV)
                    done("DVE", V.tensor_tensor(ko[:, :, 0:AD], kv, cos.unsqueeze(1).to_broadcast([P, NKV, AD]), ALU.mult), kn2.full)
                    for d0, s0 in ((0, AD // 2), (AD // 2, 0)):
                        done("DVE", V.tensor_tensor(ko[:, :, AD + d0:AD + d0 + AD // 2], kv[:, :, s0:s0 + AD // 2],
                                                    sin[:, d0:d0 + AD // 2].unsqueeze(1).to_broadcast([P, NKV, AD // 2]), ALU.mult), kn2.full, ps.free)
                    ps = banks.take()
                    wait("PE", ps.free)
                    matmuls([(ps[:], [(hT[:, k * P:(k + 1) * P], wv[:, k * 512:(k + 1) * 512]) for k in range(DC)])], ps.full, hT.free)
                    evac(v1, v1[:, t * (NKV * VW):(t + 1) * (NKV * VW)].rearrange("p (h w) -> p h w", w=VW)[:, :, 0:AD], ps,
                         ps[:].rearrange("p (h d) -> p h d", h=NKV), "ACT")
                    between()
                    for src, dst, quads in ((kn2, kT, 2), (sn, qT, 4)):
                        wait("PE", src.full)
                        for n in range(quads):
                            ps = banks.take()
                            wait("PE", ps.free)
                            for i in range(4):
                                ins = T.transpose(ps[:, i * P:(i + 1) * P], src[:, (4 * n + i) * P:(4 * n + i + 1) * P], ident[:])
                            done("PE", ins, ps.full, src.free)
                            evac(dst, dst[:].rearrange("p (h s) -> p h s", s=S)[:, 4 * n:4 * n + 4, t * P:(t + 1) * P], ps,
                                 ps[:].rearrange("p (h q) -> p h q", h=4))

                for p in range(3):
                    fetch_index(b, p)
                fetch(b, 0)
                fetch(b, 1)
                wait("ACT DVE", qT.free, kT.free, v1.free)
                layer_norm(x1[:, bass.ds(b * (TPB * D), D)])
                transpose_h()

                def second_norm():
                    layer_norm(x1[:, bass.ds(b * (TPB * D) + D, D)])
                    transpose_h()

                project(0, second_norm)
                slot(0)
                project(1, lambda: None)
                slot(1)

                wait("PE", qT.full)
                wait("PE", kT.full)
                wait("PE", v1.full)
                wait("DVE", yn.free)

                def att_scores(kh):
                    q3 = qT[:, kh * REP * S:(kh + 1) * REP * S].rearrange("p (r q) -> p r q", r=REP)
                    p0 = banks.take()
                    wait("PE", p0.free)
                    matmuls([(p0[:], [(kT[:, kh * S:kh * S + P], qT[:, kh * REP * S:(kh + 1) * REP * S])])], p0.full, kT.free, qT.free)
                    p1 = banks.take()
                    wait("PE", p1.free)
                    matmuls([(p1[:, 0:REP * P], [(kT[:, kh * S + P:(kh + 1) * S], q3[:, :, P:S])])], p1.full, kT.free, qT.free)
                    x = px.take()
                    wait("ACT", x.free)
                    wait("ACT", p0.full)
                    done("ACT", A.activation(x[:, 0:REP * S], p0[:], ACT.Tanh, scale=ASCALE / SOFTCAP), x.full, p0.free)
                    wait("ACT", p1.full)
                    done("ACT", A.activation(x[:, REP * S:], p1[:, 0:REP * P], ACT.Tanh, scale=ASCALE / SOFTCAP), x.full, p1.free)
                    wait("ACT", x.full)
                    done("ACT", A.activation(x[:], x[:], ACT.Exp, scale=SOFTCAP), x.full)
                    wait("POOL", x.full)
                    wait("POOL", tri.full)
                    d0 = x[:, 0:REP * S].rearrange("p (r q) -> p r q", r=REP)[:, :, 0:P]
                    d1 = x[:, REP * S:].rearrange("p (r q) -> p r q", r=REP)
                    for d in (d0, d1):
                        done("POOL", G.tensor_tensor(d, d, tri[:].unsqueeze(1).to_broadcast([P, REP, P]), ALU.mult), x.full)
                    return x

                def att_values(kh, x):
                    y = banks.take()
                    wait("PE", y.free)
                    wait("PE", x.full)
                    va, vb = v1[:, kh * VW:(kh + 1) * VW], v1[:, (NKV + kh) * VW:(NKV + kh + 1) * VW]
                    parts = [(y[:, r * VW:(r + 1) * VW], [(x[:, r * S:r * S + P], va)]) for r in range(REP)]
                    parts += [(y[:, (REP + r) * VW:(REP + r + 1) * VW],
                               [(x[:, r * S + P:(r + 1) * S], va), (x[:, REP * S + r * P:REP * S + (r + 1) * P], vb)])
                              for r in range(REP)]
                    matmuls(parts, y.full, x.free, v1.free)
                    rd = rden.take()
                    wait("DVE", y.full)
                    wait("DVE", rd.free)
                    yv = y[:, 0:2 * REP * VW].rearrange("p (t r w) -> p t r w", t=TPB, w=VW)
                    done("DVE", V.reciprocal(rd[:], y[:, AD:AD + (2 * REP - 1) * VW + 1:VW]), rd.full)
                    wait("DVE", rd.full)
                    done("DVE", V.tensor_tensor(
                        yn[:].rearrange("p (t r w) -> p t r w", t=TPB, w=AD)[:, :, kh * REP:(kh + 1) * REP, :], yv[:, :, :, 0:AD],
                        rd[:].rearrange("p (t r) -> p t r", t=TPB).unsqueeze(3).to_broadcast([P, TPB, REP, AD]), ALU.mult), yn.full, y.free, rd.free)

                xs_ = {0: att_scores(0)}
                for kh in range(NKV):
                    def step(kh=kh):
                        if kh + 1 < NKV:
                            xs_[kh + 1] = att_scores(kh + 1)
                        att_values(kh, xs_[kh])
                    slot(TPB + kh, step)
                slot(TPB + NKV)
                assert TPB + NKV - 3 >= NPC - 1

                wait("PE", yn.full)
                wait("PE", wao.full)
                for qt in range(TPB):
                    wait("ACT DVE", yT.free)
                    for n in range(2):
                        ps = banks.take()
                        wait("PE", ps.free)
                        for i in range(4):
                            o = qt * NH * AD + (4 * n + i) * P
                            ins = T.transpose(ps[:, i * P:(i + 1) * P], yn[:, o:o + P], ident[:])
                        done("PE", ins, ps.full, yn.free)
                        evac(yT, yT[:, n * 512:(n + 1) * 512], ps, ps[:])
                    wait("PE", psO.free)
                    wait("PE", yT.full)
                    matmuls([(psO[:], [(yT[:, k * P:(k + 1) * P], wao[:, k * D:(k + 1) * D]) for k in range(8)])], psO.full, yT.free)
                    xo = x1[:, bass.ds(b * (TPB * D) + qt * D, D)]
                    wait("DVE", psO.full)
                    done("DVE", V.tensor_tensor(xo, psO[:], xo, ALU.add), x1.full, psO.free)

        for e in ("PE", "ACT", "DVE", "POOL", "SP"):
            for o in ("PE", "ACT", "DVE", "POOL"):
                c.wait_mark(e, Mark(c.lines[o], c.lines[o].n, ()))

        TU = 2
        tiles = [dict(
            st=sb(f"st_{u}", [P, 12]), hN=sb(f"hN_{u}", [P, D]), xq=sb(f"xq_{u}", [P, D], BF16),
            xm=sb(f"xm_{u}", [P, D]), xs=sb(f"xs_{u}", [P, 8]), xqT=sb(f"xqT_{u}", [P, D], BF16),
            g=[sb(f"g{i}_{u}", [P, FT]) for i in range(NT)], t=[sb(f"t{i}_{u}", [P, FT]) for i in range(NT)],
            tops=sb(f"tops_{u}", [P, NT]), ts=sb(f"ts_{u}", [P, 4]),
            tq=[sb(f"tq{i}_{u}", [P, FT], BF16) for i in range(NT)],
            tqT=[sb(f"tqT{i}_{u}", [P, len(FCH) * P], BF16) for i in range(NT)],
            ot=sb(f"ot_{u}", [P, D])) for u in range(TU)]
        for tile in tiles:
            c.line("d_" + tile["ot"].name, 16)
            for b_ in tile["tqT"]:
                zeroed = done("POOL", G.memset(b_[:], 0.0), b_.full)
        for e in ("ACT", "DVE"):
            c.wait_mark(e, zeroed)
        wait("DVE", x1.full)

        def ffn(ti, w):
            xin = x1[:, bass.ds(ti * D, D)]
            hN, xq, xm, xs, xqT, ts, ot = (w[k] for k in ("hN", "xq", "xm", "xs", "xqT", "ts", "ot"))
            layer_norm(xin, w["st"], hN)
            yield
            quant_top(hN, hN[:], 1, xs)
            quant_scale(hN, hN[:], 1, hN, hN[:], xs)
            yield
            quant_magic(hN, hN[:], xm, xm[:])
            yield
            quant_out(hN, hN[:], xm, xm[:], xq, xq[:])
            ps = banks.take()
            wait("PE", ps.free, xq.full, identb.full)
            pb = ps[:].bitcast(BF16)
            for k in range(DC):
                ins = T.transpose(pb[:, k * P:(k + 1) * P], xq[:, k * P:(k + 1) * P], identb[:])
            done("PE", ins, ps.full, xq.free)
            wait("ACT", xqT.free)
            evac(xqT, xqT[:], ps, pb[:, 0:D], "ACT")
            yield
            wait("PE", xqT.full, qwg.full, qwu.full)
            for i, (g, t) in enumerate(zip(w["g"], w["t"])):
                o = i * FT
                pg, pu = banks.take(), banks.take()
                for ps, qw in ((pg, qwg), (pu, qwu)):
                    wait("PE", ps.free)
                    matmuls([(ps[:, 0:FT], [(xqT[:, k * P:(k + 1) * P], qw[:, k * FI + o:k * FI + o + FT]) for k in range(DC)])],
                            ps.full, xqT.free)
                wait("ACT", pg.full, xs.full, g.free)
                done("ACT", A.activation(g[:], pg[:, 0:FT], ACT.Copy, scale=xs[:, 6:7]), g.full, pg.free, xs.free)
                wait("DVE", pu.full, wsu.full, xs.full, t.free)
                done("DVE", V.scalar_tensor_tensor(t[:], pu[:, 0:FT], xs[:, 6:7], wsu[:, o:o + FT], ALU.mult, ALU.mult),
                     t.full, pu.free, xs.free)
                wait("POOL", g.full, wsg.full)
                done("POOL", G.tensor_tensor(g[:], g[:], wsg[:, o:o + FT], ALU.mult), g.full)
            yield
            tops = w["tops"]
            wait("DVE", tops.free)
            for i, (g, t) in enumerate(zip(w["g"], w["t"])):
                wait("ACT", g.full)
                done("ACT", A.activation(g[:], g[:], ACT.Silu), g.full)
                wait("DVE", g.full, t.full)
                done("DVE", V.tensor_tensor(t[:], t[:], g[:], ALU.mult), t.full, g.free)
                wait("DVE", t.full)
                done("DVE", V.tensor_reduce(tops[:, i:i + 1], t[:], AX.X, ALU.max, apply_absolute_value=True), tops.full)
            yield
            wait("DVE", tops.full, ts.free)
            done("DVE", V.tensor_reduce(ts[:, 0:1], tops[:], AX.X, ALU.max), ts.full, tops.free)
            wait("DVE", ts.full)
            done("DVE", V.reciprocal(ts[:, 3:4], ts[:, 0:1]), ts.full)
            wait("DVE", ts.full)
            done("DVE", V.tensor_scalar(ts[:, 1:2], ts[:, 3:4], FP8_MAX, None, ALU.mult), ts.full)
            done("DVE", V.tensor_scalar(ts[:, 2:3], ts[:, 0:1], 1.0 / FP8_MAX, None, ALU.mult), ts.full)
            for t in w["t"]:
                wait("ACT", ts.full, t.full)
                done("ACT", A.activation(t[:], t[:], ACT.Copy, scale=ts[:, 1:2]), t.full, ts.free)
            yield
            for g, t in zip(w["g"], w["t"]):
                quant_magic(t, t[:], g, g[:])
            yield
            wait("PE", identb.full)
            for g, t, tq, tqT in zip(w["g"], w["t"], w["tq"], w["tqT"]):
                quant_out(t, t[:], g, g[:], tq, tq[:])
                ps = banks.take()
                wait("PE", ps.free, tq.full)
                pb = ps[:].bitcast(BF16)
                for s, (o, n) in enumerate(FCH):
                    ins = T.transpose(pb[0:n, s * P:(s + 1) * P], tq[:, o:o + n], identb[:])
                done("PE", ins, ps.full, tq.free)
                wait("ACT", tqT.free)
                evac(tqT, tqT[:, 0:2 * P], ps, pb[:, 0:2 * P], "ACT")
                evac(tqT, tqT[0:FCH[2][1], 2 * P:3 * P], ps, pb[0:FCH[2][1], 2 * P:3 * P], "ACT")
            yield
            wait("PE", psO.free, qwd.full, *(x.full for x in w["tqT"]))
            matmuls([(psO[:], [(w["tqT"][k // 3][:, k % 3 * P:(k % 3 + 1) * P], qwd[:, k * D:(k + 1) * D])
                               for k in range(NFC)])], psO.full, *(x.free for x in w["tqT"]))
            wait("DVE", psO.full, ts.full, wsd.full, ot.free)
            done("DVE", V.scalar_tensor_tensor(ot[:], psO[:], ts[:, 2:3], wsd[:], ALU.mult, ALU.mult), ot.full, psO.free, ts.free)
            wait("POOL", ot.full)
            done("POOL", G.tensor_tensor(ot[:], ot[:], xin, ALU.add), ot.full)
            wait("SP", ot.full)
            done("d_" + ot.name, SP.dma_start(out.rearrange("b s d -> (b s) d")[bass.ds(ti * P, P), :], ot[:]), ot.free)

        with c.loop("ffn", NT // TU) as step:
            running = [ffn(step * TU + u, tiles[u]) for u in range(TU)]
            while running:
                running = [f for f in running if next(f, "end") != "end"]
        for tile in tiles:
            ln = c.lines["d_" + tile["ot"].name]
            c.wait_mark("SP", Mark(ln, ln.n, ()))
        return c.new


def constants():
    f = np.float32
    half = R // 2
    inv = (1.0 / 10000.0 ** (np.arange(half, dtype=np.float64) / half)).astype(f)
    ang = (np.arange(LK, dtype=f)[:, None] * inv).astype(f)
    cos, sin = np.cos(ang), np.sin(ang)
    ktab = np.concatenate([cos, cos, -sin, sin], axis=1).astype(f)
    q = np.arange(P)
    own = np.where((np.arange(GK)[None, :] % GQ) == (q[:, None] % GQ), 0.0, NEG)
    place = np.broadcast_to(np.arange(GK) // GQ, (P, GK))
    tiles = np.minimum(np.arange(NT + 1), NT) % NT
    return {
        "eye": np.eye(P, dtype=f),
        "tri": np.triu(np.ones((P, P), f)),
        "ktab": ktab,
        "qtab": np.concatenate([ktab[:S]] * B, axis=0),
        "pat": np.concatenate([own, place], axis=1).astype(f),
        "bstart": np.broadcast_to((tiles // TPB * LK).astype(f), (P, NT + 1)).copy(),
    }


NAMES = {
    "x": "x", "ctx": "ctx_2048", "itok": "itok_BxS_0_1023",
    "W_kvc": "L0_xattn_W_kvc", "W_dq": "L0_xattn_W_dq", "W_uq": "L0_xattn_W_uq", "W_qr": "L0_xattn_W_qr",
    "W_uk": "L0_xattn_W_uk", "W_kr": "L0_xattn_W_kr", "W_uv": "L0_xattn_W_uv", "W_o": "L0_xattn_W_o",
    "Wq": "L0_attn_Wq", "Wk": "L0_attn_Wk", "Wv": "L0_attn_Wv", "Wo": "L0_attn_Wo",
    "w_gate": "L0_ffn_w_gate", "w_up": "L0_ffn_w_up", "w_down": "L0_ffn_w_down",
    "d_idx": "L0_ffn_down_reorder_index",
}


def kernel(**inputs):
    import concourse.bacc as bacc
    from concourse.bass_utils import run_bass_kernel_spmd as run

    arrays = {"in_" + k: np.ascontiguousarray(inputs[v]) for k, v in NAMES.items()}
    arrays.update({"in_" + k: v for k, v in constants().items()})

    def program(plan):
        nc = bacc.Bacc("TRN2", target_bir_lowering=False, num_devices=1)
        a = {k[3:]: nc.dram_tensor(k, v.shape, mybir.dt.from_np(v.dtype), kind="ExternalInput").ap()
             for k, v in arrays.items()}
        out = nc.dram_tensor("out_0", (B, S, D), F32, kind="ExternalOutput").ap()
        return nc, build(nc, a, out, plan)

    _, plan = program({"K": {}, "opened": {}})
    nc, _ = program(plan)
    r = run(nc, [arrays], core_ids=[0])
    return r.results[0]["out_0"]
```

```python
from contextlib import ExitStack, contextmanager

import numpy as np
import concourse.bass as bass
from concourse import mybir

F32 = mybir.dt.float32
BF16 = mybir.dt.bfloat16
I32 = mybir.dt.int32
U32 = mybir.dt.uint32
ALU = mybir.AluOpType
ACT = mybir.ActivationFunctionType
AX = mybir.AxisListType

P = 128
B, S, D = 2, 256, 512
LK = 4096
NT = B * S // P
TPB = S // P
DC = D // P
H, HD, KVC, QC, R = 16, 128, 128, 192, 64
QLO, QHI = P, QC - P
LOOKBACK = 8
WIN = LOOKBACK + 1
GQ = P // H
NG = P // GQ
GK = WIN * GQ
GN = 96
XSCALE = 1.0 / float(np.sqrt(np.float32(HD + R)))
NEG = -1e30
NH, NKV, AD = 16, 8, 64
REP = NH // NKV
SOFTCAP = 50.0
ASCALE = 256.0 ** -0.5
VW = 96
FI = 1408
FT = FI // NT
FCH = [(0, 128), (128, 128), (256, 96)]
NFC = NT * len(FCH)
FP8_MAX = 448.0
EPS = 1e-5


class Line:

    def __init__(self, name, sem, step):
        self.name, self.sem, self.step, self.n, self.base = name, sem, step, 0, 0


class Mark:

    def __init__(self, line, n, path):
        self.line, self.n, self.path = line, n, path


class Counter:
    def __init__(self, nc, es, plan):
        self.nc, self.es, self.plan = nc, es, plan
        self.new = {"K": {}, "opened": {}}
        self.lines, self.gates, self.stack, self.iters = {}, [], [], {}
        self.seen = {}
        self.eng = {"PE": nc.tensor, "ACT": nc.scalar, "DVE": nc.vector, "POOL": nc.gpsimd, "SP": nc.sync}
        self.spare = es.enter_context(nc.semaphore("s_spare"))
        for e in ("PE", "ACT", "DVE", "POOL"):
            self.line(e, 1)

    def line(self, name, step, software=False):
        assert not self.stack, "a line has to be made outside of the loops"
        ln = Line(name, self.es.enter_context(self.nc.semaphore("s_" + name)), step)
        self.lines[name] = ln
        off = 0 if software else max([k.get(name, 0) for k in self.plan["K"].values()] + [0])
        if off:
            self.nc.sync.sem_inc(ln.sem, off)
        ln.base = off
        return ln

    @property
    def path(self):
        return tuple(x[0] for x in self.stack)

    def done(self, line, ins, *gates):
        ln = self.lines[line]
        ins.then_inc(ln.sem, ln.step)
        ln.n += ln.step
        m = Mark(ln, ln.n, self.path)
        for g in gates:
            g.opened[-1][line] = m
        return m

    def wait(self, engs, *gates):
        for e in engs.split():
            for g in gates:
                for d in range(len(g.opened) - 1, -1, -1):
                    for m in g.opened[d].values():
                        self.wait_mark(e, m)
                    if g.opened[d]:
                        break
                    if d > 0:
                        for m in self.plan["opened"].get(self.stack[d - 1][0], {}).get(g.name, {}).values():
                            self.wait_mark(e, m, prev=True)

    def wait_mark(self, eng, mark, prev=False):
        key = (eng, mark.line.name, mark.path, prev)
        if self.seen.get(key, -1) >= mark.n:
            return
        self.seen[key] = mark.n
        ln = self.lines[mark.line.name]
        v = mark.n + ln.base
        active = {x[0]: x[1] for x in self.stack}
        expr = None
        for lp in mark.path:
            k = self.plan["K"].get(lp, {}).get(mark.line.name, 0)
            if lp in active:
                if k:
                    expr = active[lp] * k if expr is None else expr + active[lp] * k
            else:
                v += (self.iters[lp] - 1) * k
        if prev:
            v -= self.plan["K"].get(mark.path[-1], {}).get(mark.line.name, 0)
        self.eng[eng].wait_ge(ln.sem, v if expr is None else expr + v)
        if eng == "SP":
            self.hold(eng)

    def hold(self, *engs):
        for e in engs:
            self.eng[e].sem_inc(self.spare, 1)

    @contextmanager
    def loop(self, name, n):
        if self.stack:
            self.hold(*self.eng)
        start = {k: ln.n for k, ln in self.lines.items()}
        with self.nc.Fori(0, n) as i:
            self.iters[name] = n
            self.stack.append((name, i))
            self.seen = {}
            for g in self.gates:
                g.opened.append({})
            yield i
            self.new["opened"][name] = {}
            for g in self.gates:
                inner = g.opened.pop()
                if inner:
                    self.new["opened"][name][g.name] = inner
                    g.opened[-1].update(inner)
            self.stack.pop()
            self.seen = {}
        ks = {}
        for k, ln in self.lines.items():
            d = ln.n - start.get(k, ln.n)
            ks[k] = d
            ln.n += d * (n - 1)
        self.new["K"][name] = ks


class Gate:

    def __init__(self, c, name):
        self.name = name
        self.opened = [{} for _ in range(len(c.stack) + 1)]
        c.gates.append(self)


class Buf:

    def __init__(self, c, name, t):
        self.c, self.name, self.t = c, name, t
        self.full, self.free = Gate(c, name + " full"), Gate(c, name + " free")

    def __getitem__(self, k):
        return self.t[k]


class Ring:

    def __init__(self, bufs):
        self.bufs, self.i, self.depth = bufs, 0, None

    def take(self):
        c = self.bufs[0].c
        if self.depth != c.path:
            self.depth, self.i = c.path, 0
        b = self.bufs[self.i % len(self.bufs)]
        self.i += 1
        return b


def build(nc, a, out, plan):
    with ExitStack() as es:
        c = Counter(nc, es, plan)
        T, A, V, G, SP = nc.tensor, nc.scalar, nc.vector, nc.gpsimd, nc.sync

        def sb(name, shape, dt=F32, scope=None):
            return Buf(c, name, (scope or es).enter_context(nc.sbuf_tensor(name, shape, dt)))

        banks = Ring([Buf(c, f"ps{i}", es.enter_context(nc.psum_tensor(f"ps{i}", [P, 512], F32))) for i in range(7)])
        psO = Buf(c, "psO", es.enter_context(nc.psum_tensor("psO", [P, 512], F32)))

        def dma_line(buf, software=False):
            ln = "d_" + buf.name
            if ln not in c.lines:
                c.line(ln, 16, software)
            return ln

        def load(buf, dst, src, eng="SP"):
            ln = dma_line(buf)
            h = c.eng[eng]
            with nc.allow_non_contiguous_dma(reason="strided weight or index layouts"):
                return c.done(ln, h.dma_start(dst, src), buf.full)

        wait, done = c.wait, c.done

        turn = [0]

        def evac(dst, dst_ap, bank, bank_ap, eng=None):
            if eng is None:
                eng = ("ACT", "DVE")[turn[0] % 2]
                turn[0] += 1
            wait(eng, bank.full)
            if eng == "ACT":
                ins = A.activation(dst_ap, bank_ap, ACT.Copy)
            else:
                ins = V.tensor_copy(dst_ap, bank_ap)
            return done(eng, ins, dst.full, bank.free)

        ident = sb("ident", [P, P])
        x1 = sb("x1", [P, NT * D])
        tab = sb("tab", [P, NT * P])
        half = sb("half", [P, 1])
        hN = sb("hN", [P, D])
        hT = sb("hT", [P, D])
        st = sb("st", [P, 12])
        wq = sb("wq", [P, DC * NH * AD])

        load(ident, ident[:], a["eye"])
        done("POOL", G.memset(half[:], -0.5), half.full)

        def layer_norm(xin, st=st, hN=hN):
            wait("DVE", x1.full)
            wait("POOL", half.full)
            wait("DVE", st.free)
            done("DVE", V.bn_stats(st[:, 0:6], xin), st.full)
            wait("DVE", st.full)
            c.hold("DVE")
            done("DVE", V.bn_aggr(st[:, 6:8], st[:, 0:6]), st.full)
            wait("DVE", st.full)
            done("DVE", V.tensor_scalar(st[:, 8:9], st[:, 7:8], EPS, None, ALU.add), st.full)
            wait("POOL", st.full)
            done("POOL", G.tensor_tensor(st[:, 9:10], st[:, 8:9], half[:], ALU.pow), st.full)
            wait("DVE", hN.free)
            wait("DVE", st.full)
            done("DVE", V.tensor_scalar(hN[:], xin, st[:, 6:7], st[:, 9:10], ALU.subtract, ALU.mult), hN.full, st.free, x1.free)

        def transpose_h():
            ps = banks.take()
            wait("PE", ps.free)
            wait("PE", hN.full)
            wait("PE", ident.full)
            for k in range(DC):
                ins = T.transpose(ps[:, k * P:(k + 1) * P], hN[:, k * P:(k + 1) * P], ident[:])
            done("PE", ins, ps.full, hN.free)
            wait("ACT", hT.free)
            evac(hT, hT[:], ps, ps[:], "ACT")

        def matmuls(parts, *gates):
            for o, terms in parts:
                for n, (l, rh) in enumerate(terms):
                    ins = T.matmul(o, l, rh, start=n == 0, stop=n == len(terms) - 1)
            return done("PE", ins, *gates)

        def rope(ps, heads, cs, sn, ra, rb, dst, dst_ap):
            hf = AD // 2
            xv = ps[:, 0:heads * AD].rearrange("p (h d) -> p h d", h=heads)
            av = ra[:, 0:heads * AD].rearrange("p (h d) -> p h d", h=heads)
            bv = rb[:, 0:heads * AD].rearrange("p (h d) -> p h d", h=heads)
            wait("DVE", ps.full)
            wait("DVE", tab.full)
            wait("DVE", ra.free)
            wait("DVE", rb.free)
            done("DVE", V.tensor_tensor(av, xv, cs.unsqueeze(1).to_broadcast([P, heads, AD]), ALU.mult), ra.full)
            for d0, s0 in ((0, hf), (hf, 0)):
                done("DVE", V.tensor_tensor(bv[:, :, d0:d0 + hf], xv[:, :, s0:s0 + hf],
                                              sn[:, d0:d0 + hf].unsqueeze(1).to_broadcast([P, heads, hf]), ALU.mult), rb.full, ps.free)
            wait("POOL", ra.full)
            wait("POOL", rb.full)
            done("POOL", G.tensor_tensor(dst_ap.rearrange("p (h c d) -> p h c d", h=heads, c=2),
                                       av.unsqueeze(2).to_broadcast([P, heads, 2, AD]),
                                       bv.unsqueeze(2).to_broadcast([P, heads, 2, AD]), ALU.add), dst.full, ra.free, rb.free)

        with ExitStack() as xs:
            xsb = lambda n, s, d=F32: sb(n, s, d, xs)
            g_lo = xsb("g_lo", [P, H * KVC])
            g_hi = xsb("g_hi", [P, H * KVC])
            vo = xsb("vo", [P, H * D])
            wqr_lo = xsb("wqr_lo", [P, H * R])
            wqr_hi = xsb("wqr_hi", [P, H * R])
            wdq = xsb("wdq", [P, DC * QC])
            wkvc = xsb("wkvc", [P, DC * KVC])
            wkr = xsb("wkr", [P, 2 * R])
            cg = xsb("cg", [P, WIN * D])
            rt = xsb("rt", [P, WIN * 2 * R])
            segi = xsb("segi", [P, NT], I32)
            seg = xsb("seg", [P, NT + 1])
            beg = xsb("beg", [P, NT + 1])
            upos = xsb("upos", [P, NT])
            idxc = xsb("idxc", [P, 1], I32)
            idxr = xsb("idxr", [P, 1], I32)
            bstart = xsb("bstart", [P, NT + 1])
            pat = xsb("pat", [P, 2 * GK])
            msk = xsb("msk", [P, GN], BF16)
            mtmp = xsb("mtmp", [P, 2 * GK])
            eg = xsb("eg", [P, NG * P], BF16)

            load(segi, segi[:], a["itok"].rearrange("b (t p) -> p (b t)", p=P))
            load(bstart, bstart[:], a["bstart"])
            wait("DVE", segi.full)
            wait("DVE", bstart.full)
            done("DVE", V.tensor_copy(seg[:, 0:NT], segi[:]), seg.full)
            wait("DVE", seg.full)
            done("DVE", V.tensor_copy(seg[:, NT:NT + 1], seg[:, 0:1]), seg.full)
            wait("DVE", seg.full)
            done("DVE", V.tensor_scalar(beg[:], seg[:], -float(LOOKBACK), 0.0, ALU.add, ALU.max), beg.full)
            wait("DVE", beg.full)
            done("DVE", V.tensor_scalar(beg[:], beg[:], float(LK - WIN), None, ALU.min), beg.full)
            wait("DVE", beg.full)
            done("DVE", V.tensor_tensor(upos[:], seg[:, 0:NT], beg[:, 0:NT], ALU.subtract), upos.full)

            def gather(t):
                wait("DVE", beg.full)
                wait("DVE", idxc.free)
                wait("DVE", idxr.free)
                done("DVE", V.tensor_tensor(idxc[:], beg[:, bass.ds(t, 1)], bstart[:, bass.ds(t, 1)], ALU.add), idxc.full)
                done("DVE", V.tensor_copy(idxr[:], beg[:, bass.ds(t, 1)]), idxr.full)
                for buf, idx, src in ((cg, idxc, a["ctx"].rearrange("b s d -> (b s) d")), (rt, idxr, a["ktab"])):
                    ln = dma_line(buf, software=True)
                    wait("POOL", buf.free)
                    wait("POOL", idx.full)
                    c.hold("POOL")
                    done(ln, G.indirect_dma_start(buf[:], None, src, bass.IndirectOffsetOnAxis(ap=idx[:, 0:1], axis=0)),
                         buf.full, idx.free)

            gather(0)

            done("POOL", G.memset(g_hi[:], 0.0), g_hi.full)
            done("POOL", G.memset(wqr_hi[:], 0.0), wqr_hi.full)
            done("POOL", G.memset(msk[:], 0.0), msk.full)
            wait("DVE", ident.full)
            done("DVE", V.tensor_copy(eg[:].rearrange("p (q h) -> p q h", h=H),
                                    ident[:].unsqueeze(2).to_broadcast([P, P, H])), eg.full)

            with ExitStack() as hs:
                HG, HU = 4, 8
                sets = [dict(uq_lo=sb(f"uq_lo{s}", [P, HG * HD], F32, hs), uq_hi=sb(f"uq_hi{s}", [QHI, HG * HD], F32, hs),
                             uk=sb(f"uk{s}", [KVC, HG * HD], F32, hs), uv=sb(f"uv{s}", [KVC, HG * HD], F32, hs),
                             wo=sb(f"wo{s}", [HD, HG * D], F32, hs)) for s in range(HU // HG)]
                tw = Ring([sb(f"tw{i}", [P, 2 * P + QC], F32, hs) for i in range(2)])
                wait("DVE", g_hi.full)
                for w in sets:
                    for buf in w.values():
                        dma_line(buf)
                with c.loop("heads", H // HU) as step:
                    for s, w in enumerate(sets):
                        col = step * (HU * HD) + s * HG * HD
                        for k, src in (("uq_lo", a["W_uq"][0:QLO, bass.ds(col, HG * HD)]),
                                       ("uq_hi", a["W_uq"][QLO:QC, bass.ds(col, HG * HD)]),
                                       ("uk", a["W_uk"][:, bass.ds(col, HG * HD)]),
                                       ("uv", a["W_uv"][:, bass.ds(col, HG * HD)]),
                                       ("wo", a["W_o"][bass.ds(col, HG * HD), :].rearrange("(h p) d -> p h d", p=HD))):
                            wait("SP", w[k].free)
                            load(w[k], w[k][:].rearrange("p (h d) -> p h d", h=HG) if k == "wo" else w[k][:], src)

                    def transposes(h):
                        w, e = sets[h // HG], h % HG * HD
                        ps = banks.take()
                        wait("PE", ps.free)
                        for k, o, n in (("uq_lo", 0, P), ("uq_hi", P, QHI), ("uk", QC, P), ("uv", QC + P, P)):
                            wait("PE", w[k].full)
                            c.hold("PE")
                            done("PE", T.transpose(ps[:, o:o + n], w[k][:, e:e + HD], ident[0:n, 0:n]), ps.full, w[k].free)
                        t = tw.take()
                        wait("ACT", t.free)
                        evac(t, t[:], ps, ps[:, 0:2 * P + QC], "ACT")
                        return t

                    def fold(h, t):
                        w, e = sets[h // HG], h % HG * D
                        col = step * (HU * HD) + h * HD
                        wait("PE", t.full)
                        pg = banks.take()
                        wait("PE", pg.free)
                        matmuls([(pg[:, 0:P], [(t[:, 0:P], t[:, QC:QC + P])]),
                                 (pg[0:QHI, P:2 * P], [(t[:, P:QC], t[:, QC:QC + P])])], pg.full, t.free)
                        evac(g_lo, g_lo[:, bass.ds(col, P)], pg, pg[:, 0:P], "DVE")
                        evac(g_hi, g_hi[0:QHI, bass.ds(col, P)], pg, pg[0:QHI, P:2 * P], "DVE")
                        pv = banks.take()
                        wait("PE", pv.free, w["wo"].full)
                        matmuls([(pv[:], [(t[:, QC + P:QC + 2 * P], w["wo"][:, e:e + D])])], pv.full, t.free, w["wo"].free)
                        evac(vo, vo[:, bass.ds(step * (HU * D) + h * D, D)], pv, pv[:], "DVE")

                    t = transposes(0)
                    for h in range(HU):
                        ahead = transposes(h + 1) if h + 1 < HU else None
                        fold(h, t)
                        t = ahead

            load(pat, pat[:], a["pat"])
            load(wdq, wdq[:].rearrange("p (k n) -> p k n", k=DC), a["W_dq"].rearrange("(k p) n -> p k n", p=P))
            load(x1, x1[:].rearrange("p (t d) -> p t d", t=NT), a["x"].rearrange("b (t p) d -> p (b t) d", p=P))
            load(tab, tab[:].rearrange("p (t d) -> p t d", t=NT), a["qtab"].rearrange("(t p) d -> p t d", p=P))
            load(wkvc, wkvc[:].rearrange("p (k n) -> p k n", k=DC), a["W_kvc"].rearrange("(k p) n -> p k n", p=P))
            load(wkr, wkr[:, 0:R], a["W_kr"])
            load(wkr, wkr[:, R:R + R // 2], a["W_kr"][:, R // 2:R])
            load(wkr, wkr[:, R + R // 2:2 * R], a["W_kr"][:, 0:R // 2])
            load(wqr_lo, wqr_lo[:], a["W_qr"][0:QLO, :])
            wait("SP", wqr_hi.full)
            load(wqr_hi, wqr_hi[0:QHI, :], a["W_qr"][QLO:QC, :])
            for e in ("PE", "ACT", "DVE", "POOL", "SP"):
                for o in ("PE", "ACT", "DVE"):
                    c.wait_mark(e, Mark(c.lines[o], c.lines[o].n, ()))
            load(wq, wq[:].rearrange("p (k n) -> p k n", k=DC), a["Wq"].rearrange("(k p) n -> p k n", p=P))

            qc = xsb("qc", [P, 2 * P])
            ct = Ring([xsb(f"ct{i}", [P, DC * 3 * P]) for i in range(2)])
            kc = xsb("kc", [P, NG * GK + GN - GK])
            kr = xsb("kr", [P, NG * GK + GN - GK])
            rtT = xsb("rtT", [P, WIN * P])
            kn = xsb("kn", [P, NG * KVC])
            pt = Ring([xsb(f"pt{i}", [P, 4 * P]) for i in range(2)])
            pr = Ring([xsb(f"pr{i}", [P, 4 * GK]) for i in range(4)])
            sm = Ring([xsb(f"sm{i}", [P, 12]) for i in range(4)])
            qa = xsb("qa", [P, P * H])
            qr = xsb("qr", [P, P * H])
            qn = xsb("qn", [P, H * 2 * R])
            oc = xsb("oc", [P, P * H])
            ra, rb = xsb("ra", [P, 512]), xsb("rb", [P, 512])
            done("DVE", V.memset(qc[QHI:, P:], 0.0), qc.full)
            done("POOL", G.memset(kn[:], 0.0), kn.full)
            for b_ in pt.bufs:
                done("POOL", G.memset(b_[:], 0.0), b_.full)
            for b_ in (kc, kr):
                zeroed = done("POOL", G.memset(b_[:, NG * GK:], 0.0), b_.full)

            def by_hq(buf, h0, n):
                return buf[:].rearrange("p (q h) -> p h q", h=H)[:, h0:h0 + n, :]

            def output_projection(ti):
                xin = x1[:, bass.ds(ti * D, D)]
                wait("PE", psO.free, oc.full, vo.full)
                ov = oc[:].rearrange("p (q h) -> p h q", h=H)
                matmuls([(psO[:], [(ov[:, h, :], vo[:, h * D:(h + 1) * D]) for h in range(H)])], psO.full, oc.free)
                wait("DVE", psO.full)
                done("DVE", V.tensor_tensor(xin, psO[:], xin, ALU.add), x1.full, psO.free)

            def cross_attention(ti, last=None):
                wait("PE", cg.full)
                wait("ACT DVE", kc.free)

                def window_transposes(s):
                    cb = ct.take()
                    wait("ACT DVE", cb.free)
                    for jj in range(3):
                        ps = banks.take()
                        wait("PE", ps.free)
                        for k in range(DC):
                            o = (3 * s + jj) * D + k * P
                            ins = T.transpose(ps[:, k * P:(k + 1) * P], cg[:, o:o + P], ident[:])
                        done("PE", ins, ps.full, cg.free)
                        evac(cb, cb[:].rearrange("p (k j q) -> p k j q", k=DC, j=3)[:, :, jj, :], ps,
                             ps[:].rearrange("p (k q) -> p k q", k=DC))
                    return cb

                def key_latents(s, cb):
                    ps = banks.take()
                    wait("PE", ps.free, cb.full, wkvc.full)
                    matmuls([(ps[:, 0:3 * P], [(wkvc[:, k * KVC:(k + 1) * KVC], cb[:, k * 3 * P:(k + 1) * 3 * P])
                                               for k in range(DC)])], ps.full, cb.free)
                    src = ps[:, 0:3 * P].rearrange("p (j g q) -> p j g q", j=3, g=NG)
                    dst = kc[:, 0:NG * GK].rearrange("p (g j q) -> p j g q", g=NG, j=WIN)[:, 3 * s:3 * s + 3]
                    evac(kc, dst, ps, src, "DVE")

                cb = window_transposes(0)
                layer_norm(x1[:, bass.ds(ti * D, D)])
                for s in range(WIN // 3):
                    ahead = window_transposes(s + 1) if s + 1 < WIN // 3 else None
                    if ahead is None:
                        transpose_h()
                    key_latents(s, cb)
                    cb = ahead

                wait("DVE", mtmp.free)
                wait("DVE", msk.free)
                uc = upos[:, bass.ds(ti, 1)]
                done("DVE", V.tensor_scalar(mtmp[:, 0:GK], pat[:, GK:], uc, NEG, ALU.is_gt, ALU.mult), mtmp.full)
                done("DVE", V.tensor_scalar(mtmp[:, GK:], pat[:, GK:], uc, -float(LOOKBACK), ALU.subtract, ALU.is_lt), mtmp.full)
                wait("DVE", mtmp.full)
                done("DVE", V.scalar_tensor_tensor(mtmp[:, GK:], mtmp[:, GK:], NEG, mtmp[:, 0:GK], ALU.mult, ALU.add), mtmp.full)
                wait("DVE", mtmp.full)
                done("DVE", V.tensor_tensor(msk[:, 0:GK], mtmp[:, GK:], pat[:, 0:GK], ALU.add), msk.full, mtmp.free)

                wait("PE", rt.full)
                wait("ACT DVE", rtT.free)
                for s in range(WIN // 3):
                    ps = banks.take()
                    wait("PE", ps.free)
                    for jj in range(3):
                        ins = T.transpose(ps[:, jj * P:(jj + 1) * P], rt[:, (3 * s + jj) * P:(3 * s + jj + 1) * P], ident[:])
                    done("PE", ins, ps.full, rt.free)
                    evac(rtT, rtT[:].rearrange("p (g j q) -> p j g q", g=NG, j=WIN)[:, 3 * s:3 * s + 3], ps,
                         ps[:, 0:3 * P].rearrange("p (j g q) -> p j g q", j=3, g=NG))

                gather(ti + 1)

                pq = banks.take()
                wait("PE", pq.free)
                wait("PE", hT.full)
                wait("PE", wdq.full)
                matmuls([(pq[:, 0:P], [(wdq[:, k * QC:k * QC + QLO], hT[:, k * P:(k + 1) * P]) for k in range(DC)]),
                             (pq[0:QHI, P:2 * P], [(wdq[:, k * QC + QLO:(k + 1) * QC], hT[:, k * P:(k + 1) * P])
                                                   for k in range(DC)])], pq.full, hT.free)
                wait("ACT", qc.free)
                evac(qc, qc[:, 0:P], pq, pq[:, 0:P], "ACT")
                evac(qc, qc[0:QHI, P:2 * P], pq, pq[0:QHI, P:2 * P], "ACT")

                wait("PE", qc.full)
                wait("PE", wqr_lo.full)
                wait("PE", wqr_hi.full)
                wait("POOL", qn.free)
                for n in range(2):
                    ps = banks.take()
                    wait("PE", ps.free)
                    matmuls([(ps[:], [(qc[:, 0:P], wqr_lo[:, n * 512:(n + 1) * 512]),
                                          (qc[:, P:2 * P], wqr_hi[:, n * 512:(n + 1) * 512])])], ps.full, qc.free)
                    rope(ps, 8, tab[:, bass.ds(ti * P, AD)], tab[:, bass.ds(ti * P + AD, AD)], ra, rb,
                         qn, qn[:, n * 1024:(n + 1) * 1024])

                wait("ACT DVE", qa.free)
                for n in range(4):
                    ps = banks.take()
                    wait("PE", ps.free)
                    matmuls([(ps[:, i * P:(i + 1) * P],
                                  [(g_lo[:, h * P:(h + 1) * P], qc[:, 0:P]), (g_hi[:, h * P:(h + 1) * P], qc[:, P:2 * P])])
                                 for i, h in enumerate(range(4 * n, 4 * n + 4))], ps.full, qc.free)
                    evac(qa, by_hq(qa, 4 * n, 4), ps, ps[:].rearrange("p (h q) -> p h q", h=4))

                wait("DVE", rtT.full)
                wait("PE", kc.full)
                wait("PE", wkr.full)
                wait("DVE", kr.free)
                for s in range(WIN // 3):
                    ps = banks.take()
                    wait("PE", ps.free)
                    matmuls([(ps[:, 0:3 * P], [(wkr[:], kc[:, s * 3 * P:(s + 1) * 3 * P])])], ps.full, kc.free)
                    wait("DVE", ps.full)
                    done("DVE", V.tensor_tensor(kr[:, s * 3 * P:(s + 1) * 3 * P], ps[:, 0:3 * P],
                                              rtT[:, s * 3 * P:(s + 1) * 3 * P], ALU.mult), kr.full, ps.free, rtT.free)

                wait("ACT DVE", qr.free)
                wait("PE", qn.full)
                for n in range(4):
                    ps = banks.take()
                    wait("PE", ps.free)
                    for i in range(4):
                        ins = T.transpose(ps[:, i * P:(i + 1) * P], qn[:, (4 * n + i) * P:(4 * n + i + 1) * P], ident[:])
                    done("PE", ins, ps.full, qn.free)
                    evac(qr, by_hq(qr, 4 * n, 4), ps, ps[:].rearrange("p (h q) -> p h q", h=4))

                wait("PE", qa.full)
                wait("PE", qr.full)
                wait("PE", kr.full)
                wait("PE", msk.full)
                wait("PE", eg.full)

                def scores(n):
                    ps = banks.take()
                    wait("PE", ps.free)
                    matmuls([(ps[:, i * GN:(i + 1) * GN],
                                  [(eg[:, g * P:(g + 1) * P], msk[:]),
                                   (qa[:, g * P:(g + 1) * P], kc[:, g * GK:g * GK + GN]),
                                   (qr[:, g * P:(g + 1) * P], kr[:, g * GK:g * GK + GN])])
                                 for i, g in enumerate(range(4 * n, 4 * n + 4))], ps.full, qa.free, qr.free, kc.free, kr.free, msk.free)
                    p, s = pr.take(), sm.take()
                    sv = ps[:, 0:4 * GN].rearrange("p (g k) -> p g k", g=4)[:, :, 0:GK]
                    pv = p[:].rearrange("p (g k) -> p g k", g=4)
                    wait("DVE", ps.full)
                    wait("DVE", s.free)
                    wait("DVE", p.free)
                    done("DVE", V.tensor_reduce(s[:, 0:4], sv, AX.X, ALU.max), s.full)
                    wait("DVE", s.full)
                    done("DVE", V.tensor_tensor(pv, sv, s[:, 0:4].unsqueeze(2).to_broadcast([P, 4, GK]), ALU.subtract), p.full, ps.free)
                    wait("ACT", p.full)
                    done("ACT", A.activation(p[:], p[:], ACT.Exp, scale=XSCALE), p.full)
                    wait("DVE", p.full)
                    done("DVE", V.tensor_reduce(s[:, 4:8], pv, AX.X, ALU.add), s.full)
                    wait("DVE", s.full)
                    done("DVE", V.reciprocal(s[:, 8:12], s[:, 4:8]), s.full)
                    wait("POOL", s.full)
                    wait("POOL", p.full)
                    done("POOL", G.tensor_tensor(pv, pv, s[:, 8:12].unsqueeze(2).to_broadcast([P, 4, GK]), ALU.mult), p.full, s.free)
                    return p

                def weights_transposed(n, p):
                    ps = banks.take()
                    wait("PE", ps.free, p.full)
                    for i in range(4):
                        ins = T.transpose(ps[0:GK, i * P:(i + 1) * P], p[:, i * GK:(i + 1) * GK], ident[:])
                    done("PE", ins, ps.full, p.free)
                    q = pt.take()
                    wait("ACT", q.free)
                    evac(q, q[0:GK, :], ps, ps[0:GK, :], "ACT")
                    return q

                def values(n, q):
                    ps = banks.take()
                    wait("PE", ps.free, q.full)
                    matmuls([(ps[:, i * P:(i + 1) * P], [(kn[:, (4 * n + i) * P:(4 * n + i + 1) * P],
                                                          q[:, i * P:(i + 1) * P])]) for i in range(4)], ps.full, q.free, kn.free)
                    evac(oc, oc[:, n * 512:(n + 1) * 512], ps, ps[:], "DVE")

                def key_rows(n):
                    ps = banks.take()
                    wait("PE", ps.free)
                    for i in range(4):
                        g = 4 * n + i
                        ins = T.transpose(ps[0:GK, i * P:(i + 1) * P], kc[:, g * GK:(g + 1) * GK], ident[:])
                    done("PE", ins, ps.full, kc.free)
                    evac(kn, kn[0:GK, n * 512:(n + 1) * 512], ps, ps[0:GK, :])

                if last is None:
                    for e in ("PE", "ACT", "DVE"):
                        c.wait_mark(e, zeroed)
                wait("ACT DVE", kn.free)
                probs = []
                for n in range(4):
                    probs.append(scores(n))
                    key_rows(n)
                if last is not None:
                    output_projection(last)
                wait("ACT DVE", oc.free)
                wait("PE", kn.full)
                q = weights_transposed(0, probs[0])
                for n in range(4):
                    ahead = weights_transposed(n + 1, probs[n + 1]) if n < 3 else None
                    values(n, q)
                    q = ahead

            cross_attention(0)
            with c.loop("tiles", NT - 1) as i:
                cross_attention(i + 1, i)
            output_projection(NT - 1)

        for e in ("PE", "ACT", "DVE", "POOL", "SP"):
            for o in ("PE", "ACT", "DVE", "POOL", "d_cg", "d_rt"):
                c.wait_mark(e, Mark(c.lines[o], c.lines[o].n, ()))

        qwg = sb("qwg", [P, DC * FI], BF16)
        qwu = sb("qwu", [P, DC * FI], BF16)
        qwd = sb("qwd", [P, NFC * D], BF16)
        wsg = sb("wsg", [P, FI])
        wsu = sb("wsu", [P, FI])
        wsd = sb("wsd", [P, D])
        identb = sb("identb", [P, P], BF16)
        ones = sb("ones", [P, P])
        done("DVE", V.tensor_copy(identb[:], ident[:]), identb.full)
        done("POOL", G.memset(ones[:], 1.0), ones.full)
        done("DVE", V.memset(qwd[:].rearrange("p (i s o) -> p i s o", s=3, o=D)[FCH[2][1]:, :, 2, :], 0.0), qwd.full)

        def quant_top(src, src_ap, segs, s):
            rows = src_ap.shape[0]
            sv = src_ap.rearrange("p (s n) -> p s n", s=segs)
            top, mul, inv, sc = (s[0:rows, i * 2:i * 2 + segs] for i in range(4))
            wait("DVE", src.full, s.free)
            done("DVE", V.tensor_reduce(top, sv, AX.X, ALU.max, apply_absolute_value=True), s.full)
            wait("DVE", s.full)
            done("DVE", V.reciprocal(inv, top), s.full)
            wait("DVE", s.full)
            done("DVE", V.tensor_scalar(mul, inv, FP8_MAX, None, ALU.mult), s.full)
            done("DVE", V.tensor_scalar(sc, top, 1.0 / FP8_MAX, None, ALU.mult), s.full)

        def quant_scale(src, src_ap, segs, y, y_ap, s, *gates):
            rows = src_ap.shape[0]
            sv = src_ap.rearrange("p (s n) -> p s n", s=segs)
            yv = y_ap.rearrange("p (s n) -> p s n", s=segs)
            mul = s[0:rows, 2:2 + segs]
            wait("ACT", src.full, s.full, y.free)
            for i in range(segs):
                done("ACT", A.activation(yv[:, i], sv[:, i], ACT.Copy, scale=mul[:, i:i + 1]), y.full, src.free, s.free, *gates)

        def quant_magic(y, y_ap, m, m_ap):
            wait("DVE", y.full, m.free)
            done("DVE", V.tensor_scalar(m_ap.bitcast(U32), y_ap.bitcast(U32), 0x7F800000, 0x00400000,
                                        ALU.bitwise_and, ALU.bitwise_or), m.full)
            wait("DVE", m.full)
            done("DVE", V.tensor_scalar(m_ap, m_ap, 1.5 * 2.0 ** -6, 2.0 ** 20, ALU.max, ALU.mult), m.full)
            wait("POOL", m.full, y.full)
            done("POOL", G.tensor_tensor(y_ap, y_ap, m_ap, ALU.add), y.full)

        def quant_out(y, y_ap, m, m_ap, dst, dst_ap):
            wait("DVE", y.full, m.full, dst.free)
            done("DVE", V.tensor_tensor(dst_ap, y_ap, m_ap, ALU.subtract), dst.full, y.free, m.free)

        def diagonal(s, scale_ap, rows, dg):
            wait("ACT", dg.free, s.full, ident.full)
            done("ACT", A.activation(dg[0:rows, 0:rows], ident[0:rows, 0:rows], ACT.Copy, scale=scale_ap), dg.full, s.free)

        def spread(dg, rows, dst, dst_ap):
            ps = banks.take()
            wait("PE", ps.free, dg.full, ones.full)
            matmuls([(ps[:, 0:rows], [(ones[0:rows, :], dg[0:rows, 0:rows])])], ps.full, dg.free)
            evac(dst, dst_ap, ps, ps[:, 0:rows], "ACT")

        with ExitStack() as ss:
            ssb = lambda n, s, d=F32: sb(n, s, d, ss)
            wk, wv = ssb("wk", [P, DC * NKV * AD]), ssb("wv", [P, DC * NKV * AD])
            wao = ssb("wao", [P, 8 * D])
            sn = ssb("sn", [P, NH * 2 * AD])
            kn2 = ssb("kn2", [P, NKV * P])
            sa, sbb = ssb("sa", [P, 512]), ssb("sbb", [P, 512])
            qT = ssb("qT", [P, NH * S])
            kT = ssb("kT", [P, NKV * S])
            v1 = ssb("v1", [P, TPB * NKV * VW])
            px = Ring([ssb(f"px{i}", [P, 3 * REP * P]) for i in range(3)])
            tri = ssb("tri", [P, P])
            rden = Ring([ssb(f"rden{i}", [P, 2 * REP]) for i in range(2)])
            yn = ssb("yn", [P, TPB * NH * AD])
            yT = ssb("yT", [P, NH * AD])
            wr = [ssb(f"wr{i}", [P, FI if i == len(FCH) else 2 * D]) for i in range(4)]
            wm = ssb("wm", [P, FI])
            wsc = [ssb(f"wsc{i}", [P, 8]) for i in range(3)]
            di = [ssb(f"di{i}", [P, 1], I32) for i in range(4)]
            wb = ssb("wb", [P, FI], BF16)
            dgs = [ssb(f"dg{i}", [P, P]) for i in range(2)]
            for buf in di:
                dma_line(buf)
            for buf in wr:
                if buf is wr[len(FCH)]:
                    c.line("d_" + buf.name, 16)
                else:
                    c.line("g_" + buf.name, 16, software=True)
            load(wk, wk[:].rearrange("p (k n) -> p k n", k=DC), a["Wk"].rearrange("(k p) n -> p k n", p=P))
            load(wv, wv[:].rearrange("p (k n) -> p k n", k=DC), a["Wv"].rearrange("(k p) n -> p k n", p=P))
            load(wao, wao[:].rearrange("p (k n) -> p k n", k=8), a["Wo"].rearrange("(k p) n -> p k n", p=P))
            load(tri, tri[:], a["tri"])
            v1v = v1[:].rearrange("p (x w) -> p x w", w=VW)
            done("POOL", G.memset(v1v[:, :, AD:AD + 1], 1.0), v1.full)
            vz = done("POOL", G.memset(v1v[:, :, AD + 1:], 0.0), v1.full)
            c.wait_mark("PE", vz)

            NPC = TPB * (len(FCH) + 1)

            def piece(b, p):
                ti, s = b * TPB + p // (len(FCH) + 1), p % (len(FCH) + 1)
                o, n = FCH[s] if s < len(FCH) else (None, P)
                return ti, o, n, wr[p % 4], wm, wsc[p % 3]

            def fetch_index(b, p):
                ti, o, n, _, _, _ = piece(b, p)
                if o is not None:
                    d = di[p % 4]
                    wait("SP", d.free)
                    load(d, d[0:n, :], a["d_idx"].rearrange("(n o) -> n o", o=1)[bass.ds(ti * FT + o, n), :])

            def fetch(b, p):
                ti, o, n, w, _, _ = piece(b, p)
                if o is None:
                    wait("SP", w.free)
                    done("d_" + w.name, SP.dma_start(w[:], a["w_down"][bass.ds(ti * P, P), :]), w.full)
                    return
                d = di[p % 4]
                wait("POOL", w.free, d.full)
                c.hold("POOL")
                done("g_" + w.name, G.indirect_dma_start(w[0:n, 0:2 * D], None, a["w_gu"],
                                                         bass.IndirectOffsetOnAxis(ap=d[0:n, 0:1], axis=0)), w.full)

            def piece_top(b, p):
                _, o, n, w, _, s = piece(b, p)
                quant_top(w, w[:] if o is None else w[0:n, 0:2 * D], 1 if o is None else 2, s)

            def piece_scale(b, p):
                _, o, n, w, _, s = piece(b, p)
                ap = w[:] if o is None else w[0:n, 0:2 * D]
                quant_scale(w, ap, 1 if o is None else 2, w, ap, s, *([] if o is None else [di[p % 4].free]))

            def piece_magic(b, p):
                _, o, n, w, m, _ = piece(b, p)
                e = FI if o is None else 2 * D
                quant_magic(w, w[0:n, 0:e], m, m[0:n, 0:e])

            def piece_out(b, p):
                _, o, n, w, m, s = piece(b, p)
                e = FI if o is None else 2 * D
                quant_out(w, w[0:n, 0:e], m, m[0:n, 0:e], wb, wb[0:n, 0:e])
                for i in range(1 if o is None else 2):
                    diagonal(s, s[0:n, 6 + i:7 + i], n, dgs[i])

            def piece_transpose(b, p):
                ti, o, n, _, _, s = piece(b, p)
                if o is None:
                    spread(dgs[0], P, wsd, wsd[:, bass.ds(ti * P, P)])
                    wait("PE", wb.full, identb.full)
                    for i in range(NT):
                        ps = banks.take()
                        wait("PE", ps.free)
                        pb = ps[:].bitcast(BF16)
                        for k, (o, n) in enumerate(FCH):
                            ins = T.transpose(pb[0:n, k * P:(k + 1) * P], wb[:, i * FT + o:i * FT + o + n], identb[:])
                        done("PE", ins, ps.full, wb.free)
                        qv = qwd[:].rearrange("p (c o) -> p c o", o=D)
                        pv = pb[:, 0:3 * P].rearrange("p (s o) -> p s o", s=3)
                        evac(qwd, qv[:, 3 * i:3 * i + 2, bass.ds(ti * P, P)], ps, pv[:, 0:2, :], "ACT")
                        evac(qwd, qv[0:FCH[2][1], 3 * i + 2, bass.ds(ti * P, P)], ps, pv[0:FCH[2][1], 2, :], "ACT")
                    return
                for i, (qw, ws) in enumerate(((qwg, wsg), (qwu, wsu))):
                    spread(dgs[i], n, ws, ws[:, bass.ds(ti * FT + o, n)])
                    ps = banks.take()
                    wait("PE", ps.free, wb.full, identb.full)
                    pb = ps[:].bitcast(BF16)
                    for k in range(DC):
                        ins = T.transpose(pb[:, k * P:k * P + n], wb[0:n, i * D + k * P:i * D + (k + 1) * P], identb[0:n, 0:n])
                    done("PE", ins, ps.full, wb.free)
                    evac(qw, qw[:].rearrange("p (k m) -> p k m", k=DC)[:, :, bass.ds(ti * FT + o, n)], ps,
                         pb[:, 0:DC * P].rearrange("p (k m) -> p k m", k=DC)[:, :, 0:n], "ACT")

            with c.loop("batches", B) as b:
                def slot(k, first=lambda: None, step=lambda: None):
                    first()
                    if 0 <= k - 1 < NPC:
                        piece_scale(b, k - 1)
                    if 0 <= k - 3 < NPC:
                        piece_transpose(b, k - 3)
                    if 0 <= k - 2 < NPC:
                        piece_out(b, k - 2)
                    if k + 2 < NPC:
                        fetch(b, k + 2)
                    if 0 <= k - 1 < NPC:
                        piece_magic(b, k - 1)
                    if k < NPC:
                        piece_top(b, k)
                    step()
                    if k + 3 < NPC:
                        fetch_index(b, k + 3)

                def project(t, between):
                    ti = b * TPB + t
                    cos, sin = tab[:, bass.ds(ti * P, AD)], tab[:, bass.ds(ti * P + AD, AD)]
                    wait("PE", hT.full, wq.full)
                    wait("POOL", sn.free)
                    for n in range(2):
                        ps = banks.take()
                        wait("PE", ps.free)
                        matmuls([(ps[:], [(hT[:, k * P:(k + 1) * P], wq[:, k * 1024 + n * 512:k * 1024 + (n + 1) * 512])
                                          for k in range(DC)])], ps.full, hT.free)
                        rope(ps, 8, cos, sin, sa, sbb, sn, sn[:, n * 1024:(n + 1) * 1024])
                    ps = banks.take()
                    wait("PE", ps.free, wk.full)
                    matmuls([(ps[:], [(hT[:, k * P:(k + 1) * P], wk[:, k * 512:(k + 1) * 512]) for k in range(DC)])], ps.full, hT.free)
                    wait("DVE", ps.full, kn2.free)
                    kv = ps[:].rearrange("p (h d) -> p h d", h=NKV)
                    ko = kn2[:].rearrange("p (h d) -> p h d", h=NKV)
                    done("DVE", V.tensor_tensor(ko[:, :, 0:AD], kv, cos.unsqueeze(1).to_broadcast([P, NKV, AD]), ALU.mult), kn2.full)
                    for d0, s0 in ((0, AD // 2), (AD // 2, 0)):
                        done("DVE", V.tensor_tensor(ko[:, :, AD + d0:AD + d0 + AD // 2], kv[:, :, s0:s0 + AD // 2],
                                                    sin[:, d0:d0 + AD // 2].unsqueeze(1).to_broadcast([P, NKV, AD // 2]), ALU.mult), kn2.full, ps.free)
                    ps = banks.take()
                    wait("PE", ps.free, wv.full)
                    matmuls([(ps[:], [(hT[:, k * P:(k + 1) * P], wv[:, k * 512:(k + 1) * 512]) for k in range(DC)])], ps.full, hT.free)
                    evac(v1, v1[:, t * (NKV * VW):(t + 1) * (NKV * VW)].rearrange("p (h w) -> p h w", w=VW)[:, :, 0:AD], ps,
                         ps[:].rearrange("p (h d) -> p h d", h=NKV), "ACT")
                    between()
                    for src, dst, quads in ((kn2, kT, 2), (sn, qT, 4)):
                        wait("PE", src.full)
                        for n in range(quads):
                            ps = banks.take()
                            wait("PE", ps.free)
                            for i in range(4):
                                ins = T.transpose(ps[:, i * P:(i + 1) * P], src[:, (4 * n + i) * P:(4 * n + i + 1) * P], ident[:])
                            done("PE", ins, ps.full, src.free)
                            evac(dst, dst[:].rearrange("p (h s) -> p h s", s=S)[:, 4 * n:4 * n + 4, t * P:(t + 1) * P], ps,
                                 ps[:].rearrange("p (h q) -> p h q", h=4))

                for p in range(3):
                    fetch_index(b, p)
                wait("ACT DVE", qT.free, kT.free, v1.free)
                layer_norm(x1[:, bass.ds(b * (TPB * D), D)])
                transpose_h()
                fetch(b, 0)
                fetch(b, 1)

                def second_norm():
                    layer_norm(x1[:, bass.ds(b * (TPB * D) + D, D)])
                    transpose_h()

                project(0, second_norm)
                slot(0)
                slot(1)
                project(1, lambda: slot(2))
                slot(3)

                wait("PE", qT.full)
                wait("PE", kT.full)
                wait("PE", v1.full)
                wait("DVE", yn.free)

                def att_scores(kh):
                    q3 = qT[:, kh * REP * S:(kh + 1) * REP * S].rearrange("p (r q) -> p r q", r=REP)
                    p0 = banks.take()
                    wait("PE", p0.free)
                    matmuls([(p0[:], [(kT[:, kh * S:kh * S + P], qT[:, kh * REP * S:(kh + 1) * REP * S])])], p0.full, kT.free, qT.free)
                    p1 = banks.take()
                    wait("PE", p1.free)
                    matmuls([(p1[:, 0:REP * P], [(kT[:, kh * S + P:(kh + 1) * S], q3[:, :, P:S])])], p1.full, kT.free, qT.free)
                    x = px.take()
                    wait("ACT", x.free)
                    wait("ACT", p0.full)
                    done("ACT", A.activation(x[:, 0:REP * S], p0[:], ACT.Tanh, scale=ASCALE / SOFTCAP), x.full, p0.free)
                    wait("ACT", p1.full)
                    done("ACT", A.activation(x[:, REP * S:], p1[:, 0:REP * P], ACT.Tanh, scale=ASCALE / SOFTCAP), x.full, p1.free)
                    wait("ACT", x.full)
                    done("ACT", A.activation(x[:], x[:], ACT.Exp, scale=SOFTCAP), x.full)
                    return x

                def att_mask(x):
                    wait("POOL", x.full)
                    wait("POOL", tri.full)
                    d0 = x[:, 0:REP * S].rearrange("p (r q) -> p r q", r=REP)[:, :, 0:P]
                    d1 = x[:, REP * S:].rearrange("p (r q) -> p r q", r=REP)
                    for d in (d0, d1):
                        done("POOL", G.tensor_tensor(d, d, tri[:].unsqueeze(1).to_broadcast([P, REP, P]), ALU.mult), x.full)

                def att_values(kh, x):
                    y = banks.take()
                    wait("PE", y.free)
                    wait("PE", x.full)
                    va, vb = v1[:, kh * VW:(kh + 1) * VW], v1[:, (NKV + kh) * VW:(NKV + kh + 1) * VW]
                    parts = [(y[:, r * VW:(r + 1) * VW], [(x[:, r * S:r * S + P], va)]) for r in range(REP)]
                    parts += [(y[:, (REP + r) * VW:(REP + r + 1) * VW],
                               [(x[:, r * S + P:(r + 1) * S], va), (x[:, REP * S + r * P:REP * S + (r + 1) * P], vb)])
                              for r in range(REP)]
                    matmuls(parts, y.full, x.free, v1.free)
                    rd = rden.take()
                    wait("DVE", y.full)
                    wait("DVE", rd.free)
                    yv = y[:, 0:2 * REP * VW].rearrange("p (t r w) -> p t r w", t=TPB, w=VW)
                    done("DVE", V.reciprocal(rd[:], y[:, AD:AD + (2 * REP - 1) * VW + 1:VW]), rd.full)
                    wait("DVE", rd.full)
                    done("DVE", V.tensor_tensor(
                        yn[:].rearrange("p (t r w) -> p t r w", t=TPB, w=AD)[:, :, kh * REP:(kh + 1) * REP, :], yv[:, :, :, 0:AD],
                        rd[:].rearrange("p (t r) -> p t r", t=TPB).unsqueeze(3).to_broadcast([P, TPB, REP, AD]), ALU.mult), yn.full, y.free, rd.free)

                heads = [att_scores(0), att_scores(1)]
                att_mask(heads[0])
                for kh in range(NKV):
                    def first():
                        if kh + 1 < NKV:
                            att_mask(heads[kh + 1])

                    def step():
                        if kh + 2 < NKV:
                            heads.append(att_scores(kh + 2))
                        att_values(kh, heads[kh])

                    slot(2 * TPB + kh, first, step)
                assert 2 * TPB + NKV - 1 - 3 >= NPC - 1

                wait("PE", yn.full, wao.full)
                turned = (yT, kn2)
                for qt, y in enumerate(turned):
                    wait("ACT DVE", y.free)
                    for n in range(2):
                        ps = banks.take()
                        wait("PE", ps.free)
                        for i in range(4):
                            o = qt * NH * AD + (4 * n + i) * P
                            ins = T.transpose(ps[:, i * P:(i + 1) * P], yn[:, o:o + P], ident[:])
                        done("PE", ins, ps.full, yn.free)
                        evac(y, y[:, n * 512:(n + 1) * 512], ps, ps[:])
                for qt, y in enumerate(turned):
                    ps = banks.take()
                    wait("PE", ps.free, y.full)
                    matmuls([(ps[:], [(y[:, k * P:(k + 1) * P], wao[:, k * D:(k + 1) * D]) for k in range(8)])], ps.full, y.free)
                    xo = x1[:, bass.ds(b * (TPB * D) + qt * D, D)]
                    wait("DVE", ps.full)
                    done("DVE", V.tensor_tensor(xo, ps[:], xo, ALU.add), x1.full, ps.free)

        for e in ("PE", "ACT", "DVE", "POOL", "SP"):
            for o in ("PE", "ACT", "DVE", "POOL"):
                c.wait_mark(e, Mark(c.lines[o], c.lines[o].n, ()))

        TU = 2
        tiles = [dict(
            st=sb(f"st_{u}", [P, 12]), hN=sb(f"hN_{u}", [P, D]), xq=sb(f"xq_{u}", [P, D], BF16),
            xm=sb(f"xm_{u}", [P, D]), xs=sb(f"xs_{u}", [P, 8]), xqT=sb(f"xqT_{u}", [P, D], BF16),
            g=[sb(f"g{i}_{u}", [P, FT]) for i in range(NT)], t=[sb(f"t{i}_{u}", [P, FT]) for i in range(NT)],
            tops=sb(f"tops_{u}", [P, NT]), ts=sb(f"ts_{u}", [P, 4]),
            tq=[sb(f"tq{i}_{u}", [P, FT], BF16) for i in range(NT)],
            tqT=[sb(f"tqT{i}_{u}", [P, len(FCH) * P], BF16) for i in range(NT)],
            ot=sb(f"ot_{u}", [P, D])) for u in range(TU)]
        for tile in tiles:
            c.line("d_" + tile["ot"].name, 16)
            for b_ in tile["tqT"]:
                zeroed = done("DVE", V.memset(b_[FCH[2][1]:, 2 * P:], 0.0), b_.full)
        c.wait_mark("PE", zeroed)
        wait("DVE", x1.full)

        def ffn(ti, w):
            xin = x1[:, bass.ds(ti * D, D)]
            hN, xq, xm, xs, xqT, ts, ot = (w[k] for k in ("hN", "xq", "xm", "xs", "xqT", "ts", "ot"))
            layer_norm(xin, w["st"], hN)
            yield
            quant_top(hN, hN[:], 1, xs)
            quant_scale(hN, hN[:], 1, hN, hN[:], xs)
            yield
            quant_magic(hN, hN[:], xm, xm[:])
            yield
            quant_out(hN, hN[:], xm, xm[:], xq, xq[:])
            ps = banks.take()
            wait("PE", ps.free, xq.full, identb.full)
            pb = ps[:].bitcast(BF16)
            for k in range(DC):
                ins = T.transpose(pb[:, k * P:(k + 1) * P], xq[:, k * P:(k + 1) * P], identb[:])
            done("PE", ins, ps.full, xq.free)
            wait("ACT", xqT.free)
            evac(xqT, xqT[:], ps, pb[:, 0:D], "ACT")
            yield
            wait("PE", xqT.full, qwg.full, qwu.full)

            def gate_up(i):
                g, t, o = w["g"][i], w["t"][i], i * FT
                pg, pu = banks.take(), banks.take()
                for ps, qw in ((pg, qwg), (pu, qwu)):
                    wait("PE", ps.free)
                    matmuls([(ps[:, 0:FT], [(xqT[:, k * P:(k + 1) * P], qw[:, k * FI + o:k * FI + o + FT]) for k in range(DC)])],
                            ps.full, xqT.free)
                wait("ACT", pg.full, xs.full, g.free)
                done("ACT", A.activation(g[:], pg[:, 0:FT], ACT.Copy, scale=xs[:, 6:7]), g.full, pg.free, xs.free)
                wait("DVE", pu.full, wsu.full, xs.full, t.free)
                done("DVE", V.scalar_tensor_tensor(t[:], pu[:, 0:FT], xs[:, 6:7], wsu[:, o:o + FT], ALU.mult, ALU.mult),
                     t.full, pu.free, xs.free)
                wait("POOL", g.full, wsg.full)
                done("POOL", G.tensor_tensor(g[:], g[:], wsg[:, o:o + FT], ALU.mult), g.full)

            def gated(i):
                g, t = w["g"][i], w["t"][i]
                wait("ACT", g.full)
                done("ACT", A.activation(g[:], g[:], ACT.Silu), g.full)
                wait("DVE", g.full, t.full)
                done("DVE", V.tensor_tensor(t[:], t[:], g[:], ALU.mult), t.full, g.free)
                wait("DVE", t.full)
                done("DVE", V.tensor_reduce(tops[:, i:i + 1], t[:], AX.X, ALU.max, apply_absolute_value=True), tops.full)

            tops = w["tops"]
            wait("DVE", tops.free)
            for i in range(NT):
                gate_up(i)
                if i:
                    gated(i - 1)
                yield
            gated(NT - 1)
            yield
            wait("DVE", tops.full, ts.free)
            done("DVE", V.tensor_reduce(ts[:, 0:1], tops[:], AX.X, ALU.max), ts.full, tops.free)
            wait("DVE", ts.full)
            done("DVE", V.reciprocal(ts[:, 3:4], ts[:, 0:1]), ts.full)
            wait("DVE", ts.full)
            done("DVE", V.tensor_scalar(ts[:, 1:2], ts[:, 3:4], FP8_MAX, None, ALU.mult), ts.full)
            done("DVE", V.tensor_scalar(ts[:, 2:3], ts[:, 0:1], 1.0 / FP8_MAX, None, ALU.mult), ts.full)
            for t in w["t"]:
                wait("ACT", ts.full, t.full)
                done("ACT", A.activation(t[:], t[:], ACT.Copy, scale=ts[:, 1:2]), t.full, ts.free)
            yield
            for g, t in zip(w["g"], w["t"]):
                quant_magic(t, t[:], g, g[:])
            yield
            wait("PE", identb.full)
            for g, t, tq, tqT in zip(w["g"], w["t"], w["tq"], w["tqT"]):
                quant_out(t, t[:], g, g[:], tq, tq[:])
                ps = banks.take()
                wait("PE", ps.free, tq.full)
                pb = ps[:].bitcast(BF16)
                for s, (o, n) in enumerate(FCH):
                    ins = T.transpose(pb[0:n, s * P:(s + 1) * P], tq[:, o:o + n], identb[:])
                done("PE", ins, ps.full, tq.free)
                wait("ACT", tqT.free)
                evac(tqT, tqT[:, 0:2 * P], ps, pb[:, 0:2 * P], "ACT")
                evac(tqT, tqT[0:FCH[2][1], 2 * P:3 * P], ps, pb[0:FCH[2][1], 2 * P:3 * P], "ACT")
            while unfinished:
                unfinished.pop()()
            wait("PE", psO.free, qwd.full, *(x.full for x in w["tqT"]))
            matmuls([(psO[:], [(w["tqT"][k // 3][:, k % 3 * P:(k % 3 + 1) * P], qwd[:, k * D:(k + 1) * D])
                               for k in range(NFC)])], psO.full, *(x.free for x in w["tqT"]))

            def finish():
                wait("DVE", psO.full, ts.full, wsd.full, ot.free)
                done("DVE", V.scalar_tensor_tensor(ot[:], psO[:], ts[:, 2:3], wsd[:], ALU.mult, ALU.mult), ot.full, psO.free, ts.free)
                wait("DVE", ot.full)
                done("DVE", V.tensor_tensor(ot[:], ot[:], xin, ALU.add), ot.full)
                wait("SP", ot.full)
                done("d_" + ot.name, SP.dma_start(out.rearrange("b s d -> (b s) d")[bass.ds(ti * P, P), :], ot[:]), ot.free)

            unfinished.append(finish)

        unfinished = []
        with c.loop("ffn", NT // TU) as step:
            running = [ffn(step * TU + u, tiles[u]) for u in range(TU)]
            while running:
                running = [f for f in running if next(f, "end") != "end"]
            while unfinished:
                unfinished.pop()()
        for tile in tiles:
            ln = c.lines["d_" + tile["ot"].name]
            c.wait_mark("SP", Mark(ln, ln.n, ()))
        return c.new


def constants():
    f = np.float32
    half = R // 2
    inv = (1.0 / 10000.0 ** (np.arange(half, dtype=np.float64) / half)).astype(f)
    ang = (np.arange(LK, dtype=f)[:, None] * inv).astype(f)
    cos, sin = np.cos(ang), np.sin(ang)
    ktab = np.concatenate([cos, cos, -sin, sin], axis=1).astype(f)
    q = np.arange(P)
    own = np.where((np.arange(GK)[None, :] % GQ) == (q[:, None] % GQ), 0.0, NEG)
    place = np.broadcast_to(np.arange(GK) // GQ, (P, GK))
    tiles = np.minimum(np.arange(NT + 1), NT) % NT
    return {
        "eye": np.eye(P, dtype=f),
        "tri": np.triu(np.ones((P, P), f)),
        "ktab": ktab,
        "qtab": np.concatenate([ktab[:S]] * B, axis=0),
        "pat": np.concatenate([own, place], axis=1).astype(f),
        "bstart": np.broadcast_to((tiles // TPB * LK).astype(f), (P, NT + 1)).copy(),
    }


NAMES = {
    "x": "x", "ctx": "ctx_2048", "itok": "itok_BxS_0_1023",
    "W_kvc": "L0_xattn_W_kvc", "W_dq": "L0_xattn_W_dq", "W_uq": "L0_xattn_W_uq", "W_qr": "L0_xattn_W_qr",
    "W_uk": "L0_xattn_W_uk", "W_kr": "L0_xattn_W_kr", "W_uv": "L0_xattn_W_uv", "W_o": "L0_xattn_W_o",
    "Wq": "L0_attn_Wq", "Wk": "L0_attn_Wk", "Wv": "L0_attn_Wv", "Wo": "L0_attn_Wo",
    "w_down": "L0_ffn_w_down",
    "d_idx": "L0_ffn_down_reorder_index",
}


def kernel(**inputs):
    import concourse.bacc as bacc
    from concourse.bass_utils import run_bass_kernel_spmd as run

    arrays = {"in_" + k: np.ascontiguousarray(inputs[v]) for k, v in NAMES.items()}
    arrays["in_w_gu"] = np.concatenate([inputs["L0_ffn_w_gate"], inputs["L0_ffn_w_up"]], axis=1)
    arrays.update({"in_" + k: v for k, v in constants().items()})

    def program(plan):
        nc = bacc.Bacc("TRN2", target_bir_lowering=False, num_devices=1)
        a = {k[3:]: nc.dram_tensor(k, v.shape, mybir.dt.from_np(v.dtype), kind="ExternalInput").ap()
             for k, v in arrays.items()}
        out = nc.dram_tensor("out_0", (B, S, D), F32, kind="ExternalOutput").ap()
        return nc, build(nc, a, out, plan)

    _, plan = program({"K": {}, "opened": {}})
    nc, _ = program(plan)
    r = run(nc, [arrays], core_ids=[0])
    return r.results[0]["out_0"]
```
